# Optimizing a Trainium2 kernel written in Bass

```python
import numpy as np
import jax
import jax.numpy as jnp

def _softmax(x, axis=-1):
    return jax.nn.softmax(x, axis=axis)

def _gelu(x):
    return jax.nn.gelu(x, approximate=True)

def _silu(x):
    return jax.nn.silu(x)

def _sigmoid(x):
    return jax.nn.sigmoid(x)

def _layernorm(x, axis=-1, eps=1e-05):
    m = jnp.mean(x, axis=axis, keepdims=True)
    v = jnp.var(x, axis=axis, keepdims=True)
    return (x - m) / jnp.sqrt(v + eps)

def _scatter_add(tgt, idx, src, axis=0):
    return tgt.at[idx].add(src)

def _segment_sum(src, seg, n):
    return jax.ops.segment_sum(src, seg, n)
kernel_name = 'mk_dlrm_tower_d1_rec_r8_06a54d'

def setup_inputs(seed: int=0):
    np.random.seed(seed)
    _w = jnp.asarray

    def _rec_inputs():
        import jax
        import jax.numpy as jnp
        _tk = jax.random.key(seed)
        ids = jnp.stack([jax.random.randint(jax.random.fold_in(_tk, 200 + f), (2048,), 0, v, jnp.int32) for f, v in enumerate([1000, 12500, 125000, 12500, 12500, 1250, 12500, 12500, 1250, 1000, 1250, 1250, 12500, 125000, 12500, 125000, 1000, 1000, 12500, 1250, 1000, 1250, 1250, 1000, 1000, 1250])], axis=1)
        tbl_0 = 0.05 * jax.random.normal(jax.random.fold_in(_tk, 500 + 0), (1000, 64), jnp.float32)
        tbl_1 = 0.05 * jax.random.normal(jax.random.fold_in(_tk, 500 + 1), (12500, 64), jnp.float32)
        tbl_2 = 0.05 * jax.random.normal(jax.random.fold_in(_tk, 500 + 2), (125000, 64), jnp.float32)
        tbl_3 = 0.05 * jax.random.normal(jax.random.fold_in(_tk, 500 + 3), (12500, 64), jnp.float32)
        tbl_4 = 0.05 * jax.random.normal(jax.random.fold_in(_tk, 500 + 4), (12500, 64), jnp.float32)
        tbl_5 = 0.05 * jax.random.normal(jax.random.fold_in(_tk, 500 + 5), (1250, 64), jnp.float32)
        tbl_6 = 0.05 * jax.random.normal(jax.random.fold_in(_tk, 500 + 6), (12500, 64), jnp.float32)
        tbl_7 = 0.05 * jax.random.normal(jax.random.fold_in(_tk, 500 + 7), (12500, 64), jnp.float32)
        tbl_8 = 0.05 * jax.random.normal(jax.random.fold_in(_tk, 500 + 8), (1250, 64), jnp.float32)
        tbl_9 = 0.05 * jax.random.normal(jax.random.fold_in(_tk, 500 + 9), (1000, 64), jnp.float32)
        tbl_10 = 0.05 * jax.random.normal(jax.random.fold_in(_tk, 500 + 10), (1250, 64), jnp.float32)
        tbl_11 = 0.05 * jax.random.normal(jax.random.fold_in(_tk, 500 + 11), (1250, 64), jnp.float32)
        tbl_12 = 0.05 * jax.random.normal(jax.random.fold_in(_tk, 500 + 12), (12500, 64), jnp.float32)
        tbl_13 = 0.05 * jax.random.normal(jax.random.fold_in(_tk, 500 + 13), (125000, 64), jnp.float32)
        tbl_14 = 0.05 * jax.random.normal(jax.random.fold_in(_tk, 500 + 14), (12500, 64), jnp.float32)
        tbl_15 = 0.05 * jax.random.normal(jax.random.fold_in(_tk, 500 + 15), (125000, 64), jnp.float32)
        tbl_16 = 0.05 * jax.random.normal(jax.random.fold_in(_tk, 500 + 16), (1000, 64), jnp.float32)
        tbl_17 = 0.05 * jax.random.normal(jax.random.fold_in(_tk, 500 + 17), (1000, 64), jnp.float32)
        tbl_18 = 0.05 * jax.random.normal(jax.random.fold_in(_tk, 500 + 18), (12500, 64), jnp.float32)
        tbl_19 = 0.05 * jax.random.normal(jax.random.fold_in(_tk, 500 + 19), (1250, 64), jnp.float32)
        tbl_20 = 0.05 * jax.random.normal(jax.random.fold_in(_tk, 500 + 20), (1000, 64), jnp.float32)
        tbl_21 = 0.05 * jax.random.normal(jax.random.fold_in(_tk, 500 + 21), (1250, 64), jnp.float32)
        tbl_22 = 0.05 * jax.random.normal(jax.random.fold_in(_tk, 500 + 22), (1250, 64), jnp.float32)
        tbl_23 = 0.05 * jax.random.normal(jax.random.fold_in(_tk, 500 + 23), (1000, 64), jnp.float32)
        tbl_24 = 0.05 * jax.random.normal(jax.random.fold_in(_tk, 500 + 24), (1000, 64), jnp.float32)
        tbl_25 = 0.05 * jax.random.normal(jax.random.fold_in(_tk, 500 + 25), (1250, 64), jnp.float32)
        _rk = jax.random.fold_in(_tk, 7)
        r_dense_t = 7.22013e-05 + 1.00017 * jax.random.normal(jax.random.fold_in(_rk, 101), (2048, 256), jnp.float32)
        W_top1 = 0.0360844 * jax.random.normal(jax.random.fold_in(_tk, 801), (768, 512), jnp.float32)
        W_top2 = 0.0441942 * jax.random.normal(jax.random.fold_in(_tk, 802), (512, 256), jnp.float32)
        W_top3 = 0.0625 * jax.random.normal(jax.random.fold_in(_tk, 803), (256, 1), jnp.float32)
        b_top1 = jnp.zeros((512,), jnp.float32)
        b_top2 = jnp.zeros((256,), jnp.float32)
        return (r_dense_t, ids, tbl_0, tbl_1, tbl_2, tbl_3, tbl_4, tbl_5, tbl_6, tbl_7, tbl_8, tbl_9, tbl_10, tbl_11, tbl_12, tbl_13, tbl_14, tbl_15, tbl_16, tbl_17, tbl_18, tbl_19, tbl_20, tbl_21, tbl_22, tbl_23, tbl_24, tbl_25, W_top1, b_top1, W_top2, b_top2, W_top3)
    r_dense_t, ids, tbl_0, tbl_1, tbl_2, tbl_3, tbl_4, tbl_5, tbl_6, tbl_7, tbl_8, tbl_9, tbl_10, tbl_11, tbl_12, tbl_13, tbl_14, tbl_15, tbl_16, tbl_17, tbl_18, tbl_19, tbl_20, tbl_21, tbl_22, tbl_23, tbl_24, tbl_25, W_top1, b_top1, W_top2, b_top2, W_top3 = _rec_inputs()

    def _L0_rec_setup():
        import jax, jax.numpy as jnp
        import numpy as np
        EPS = 1e-05
        NI = 33
        TRIL_I, TRIL_J = np.tril_indices(NI, k=-1)

        def layer_norm(x, g, b):
            m = jnp.mean(x, axis=-1, keepdims=True)
            v = jnp.mean(jnp.square(x - m), axis=-1, keepdims=True)
            return (x - m) * jax.lax.rsqrt(v + EPS) * g + b
        key = jax.random.key(seed)
        ks = jax.random.split(key, 8)
        B, D_DENSE, N_SP, D_SP = (4096, 256, 26, 64)
        E, PROJ, MAXD, NFLAT = (128, 32, 512, 528)
        dense_t = jax.random.normal(ks[0], (B, D_DENSE), dtype=jnp.float32)
        sparse_t = jax.random.normal(ks[1], (B, N_SP, D_SP), dtype=jnp.float32)
        Wd = jax.random.normal(ks[2], (E, D_DENSE), dtype=jnp.float32) / np.sqrt(D_DENSE)
        Ws = jax.random.normal(ks[3], (E, D_SP), dtype=jnp.float32) / np.sqrt(D_SP)
        Wsi = jax.random.normal(ks[4], (PROJ, N_SP), dtype=jnp.float32) / np.sqrt(N_SP)
        Wl = jax.random.normal(ks[5], (MAXD, NFLAT), dtype=jnp.float32) / np.sqrt(NFLAT)
        gd = jnp.ones((E,), jnp.float32)
        bd = jnp.zeros((E,), jnp.float32)
        gs = jnp.ones((E,), jnp.float32)
        bs = jnp.zeros((E,), jnp.float32)
        gsi = jnp.ones((PROJ,), jnp.float32)
        bsi = jnp.zeros((PROJ,), jnp.float32)
        gl = jnp.ones((MAXD,), jnp.float32)
        bl = jnp.zeros((MAXD,), jnp.float32)
        return {'dense_t': dense_t, 'sparse_t': sparse_t, 'Wd': Wd, 'gd': gd, 'bd': bd, 'Ws': Ws, 'gs': gs, 'bs': bs, 'Wsi': Wsi, 'gsi': gsi, 'bsi': bsi, 'Wl': Wl, 'gl': gl, 'bl': bl, 'dims_in_use': 384}
    _L0_rec_all = _L0_rec_setup()
    _L0_rec_in = {k: v for k, v in _L0_rec_all.items() if k in ('Wd', 'gd', 'bd', 'Ws', 'gs', 'bs', 'Wsi', 'gsi', 'bsi', 'Wl', 'gl', 'bl')}
    del _L0_rec_all
    return {'r_dense_t': r_dense_t, 'ids': ids, 'tbl_0': tbl_0, 'tbl_1': tbl_1, 'tbl_2': tbl_2, 'tbl_3': tbl_3, 'tbl_4': tbl_4, 'tbl_5': tbl_5, 'tbl_6': tbl_6, 'tbl_7': tbl_7, 'tbl_8': tbl_8, 'tbl_9': tbl_9, 'tbl_10': tbl_10, 'tbl_11': tbl_11, 'tbl_12': tbl_12, 'tbl_13': tbl_13, 'tbl_14': tbl_14, 'tbl_15': tbl_15, 'tbl_16': tbl_16, 'tbl_17': tbl_17, 'tbl_18': tbl_18, 'tbl_19': tbl_19, 'tbl_20': tbl_20, 'tbl_21': tbl_21, 'tbl_22': tbl_22, 'tbl_23': tbl_23, 'tbl_24': tbl_24, 'tbl_25': tbl_25, 'W_top1': W_top1, 'b_top1': b_top1, 'W_top2': W_top2, 'b_top2': b_top2, 'W_top3': W_top3, 'L0_rec_Wd': _L0_rec_in['Wd'], 'L0_rec_gd': _L0_rec_in['gd'], 'L0_rec_bd': _L0_rec_in['bd'], 'L0_rec_Ws': _L0_rec_in['Ws'], 'L0_rec_gs': _L0_rec_in['gs'], 'L0_rec_bs': _L0_rec_in['bs'], 'L0_rec_Wsi': _L0_rec_in['Wsi'], 'L0_rec_gsi': _L0_rec_in['gsi'], 'L0_rec_bsi': _L0_rec_in['bsi'], 'L0_rec_Wl': _L0_rec_in['Wl'], 'L0_rec_gl': _L0_rec_in['gl'], 'L0_rec_bl': _L0_rec_in['bl']}

def reference(r_dense_t, ids, tbl_0, tbl_1, tbl_2, tbl_3, tbl_4, tbl_5, tbl_6, tbl_7, tbl_8, tbl_9, tbl_10, tbl_11, tbl_12, tbl_13, tbl_14, tbl_15, tbl_16, tbl_17, tbl_18, tbl_19, tbl_20, tbl_21, tbl_22, tbl_23, tbl_24, tbl_25, W_top1, b_top1, W_top2, b_top2, W_top3, L0_rec_Wd, L0_rec_gd, L0_rec_bd, L0_rec_Ws, L0_rec_gs, L0_rec_bs, L0_rec_Wsi, L0_rec_gsi, L0_rec_bsi, L0_rec_Wl, L0_rec_gl, L0_rec_bl):
    import jax
    import jax.numpy as jnp

    def _L0_rec_ref(dense_t, sparse_t, Wd, gd, bd, Ws, gs, bs, Wsi, gsi, bsi, Wl, gl, bl, dims_in_use):
        import jax, jax.numpy as jnp
        import numpy as np
        EPS = 1e-05
        NI = 33
        TRIL_I, TRIL_J = np.tril_indices(NI, k=-1)

        def layer_norm(x, g, b):
            m = jnp.mean(x, axis=-1, keepdims=True)
            v = jnp.mean(jnp.square(x - m), axis=-1, keepdims=True)
            return (x - m) * jax.lax.rsqrt(v + EPS) * g + b
        x = layer_norm(dense_t @ Wd.T, gd, bd)
        y = layer_norm(jnp.einsum('bnd,ed->bne', sparse_t, Ws), gs, bs)
        y = jnp.einsum('bne,pn->bep', y, Wsi)
        y = layer_norm(y, gsi, bsi)
        y = jnp.swapaxes(y, 1, 2)
        T = jnp.concatenate([x[:, None, :], y], axis=1)
        Z = jnp.einsum('bnd,bmd->bnm', T, T)
        Zflat = Z[:, TRIL_I, TRIL_J]
        out = layer_norm(Zflat @ Wl.T, gl, bl)
        maxd = out.shape[-1]
        mask = (jnp.arange(maxd) < dims_in_use).astype(out.dtype)
        return out * mask
    e = jnp.stack([tbl_0[ids[:, 0]], tbl_1[ids[:, 1]], tbl_2[ids[:, 2]], tbl_3[ids[:, 3]], tbl_4[ids[:, 4]], tbl_5[ids[:, 5]], tbl_6[ids[:, 6]], tbl_7[ids[:, 7]], tbl_8[ids[:, 8]], tbl_9[ids[:, 9]], tbl_10[ids[:, 10]], tbl_11[ids[:, 11]], tbl_12[ids[:, 12]], tbl_13[ids[:, 13]], tbl_14[ids[:, 14]], tbl_15[ids[:, 15]], tbl_16[ids[:, 16]], tbl_17[ids[:, 17]], tbl_18[ids[:, 18]], tbl_19[ids[:, 19]], tbl_20[ids[:, 20]], tbl_21[ids[:, 21]], tbl_22[ids[:, 22]], tbl_23[ids[:, 23]], tbl_24[ids[:, 24]], tbl_25[ids[:, 25]]], axis=1)
    z = _L0_rec_ref(r_dense_t, e, L0_rec_Wd, L0_rec_gd, L0_rec_bd, L0_rec_Ws, L0_rec_gs, L0_rec_bs, L0_rec_Wsi, L0_rec_gsi, L0_rec_bsi, L0_rec_Wl, L0_rec_gl, L0_rec_bl, 384)
    z = z.reshape(z.shape[0], -1)
    h = jnp.concatenate([z, r_dense_t], axis=1)
    h = jnp.maximum(h @ W_top1 + b_top1, 0.0)
    h = jnp.maximum(h @ W_top2 + b_top2, 0.0)
    y = h @ W_top3
    return y

_drawn_inputs = setup_inputs


def setup_inputs(seed=0):
    import zlib

    import numpy as np

    out = dict(_drawn_inputs(seed))
    spreads = {'b_top1': (0.0, 0.1),
     'b_top2': (0.0, 0.1),
     'L0_rec_gd': (1.0, 0.6),
     'L0_rec_bd': (0.0, 0.8),
     'L0_rec_gs': (1.0, 0.6),
     'L0_rec_bs': (0.0, 0.1),
     'L0_rec_gsi': (1.0, 0.2),
     'L0_rec_bsi': (0.0, 0.1),
     'L0_rec_gl': (1.0, 0.2),
     'L0_rec_bl': (0.0, 0.1)}
    factors = {}
    for name, (base, spread) in spreads.items():
        noise = np.random.default_rng([zlib.crc32(name.encode()), seed]).standard_normal(out[name].shape)
        drawn = base * np.exp(spread * noise) if base else spread * noise
        out[name] = jnp.asarray(drawn.astype(out[name].dtype))
    for name, factor in factors.items():
        out[name] = (out[name] * factor).astype(out[name].dtype)
    return out
```

```python
import numpy as np
import concourse.bass as bass
from concourse import mybir
from contextlib import ExitStack

F32 = mybir.dt.float32
AFFINE_ACT = ((range(0, 2), range(2, 4)), (range(4, 6), range(6, 10)), (range(10, 12), range(12, 16)), (range(16, 18), range(18, 20)))
AFFINE_DVE = (range(20, 23), range(23, 26), range(26, 29), range(29, 32))
BF16 = mybir.dt.bfloat16
I32 = mybir.dt.int32
ACT = mybir.ActivationFunctionType
ALU = mybir.AluOpType
AX = mybir.AxisListType.X

N_SAMPLES, N_TABLES, D_EMB = 2048, 26, 64
D_DENSE, D_OUT, N_PROJ = 256, 128, 32
D_PAIR, D_USED = 512, 384
D_H1, D_H2 = 512, 256
P = 128
TILE = P
TILES = N_SAMPLES // TILE
GRP = 4
GROUPS = TILE // GRP
ROWS = GRP * N_TABLES
CHUNKS = 4
CG = GROUPS // CHUNKS
CP = CG // 2
QG = 4
QC = N_PROJ // QG
EPS = 1e-5
PARTS = 9
LAST_LAG = 5
STEPS = TILES + LAST_LAG


class Step:

    def __init__(self, k, u):
        self.k, self.u, self.fixed = k, u, isinstance(k, int)

    def live(self, lag):
        return not self.fixed or 0 <= 2 * self.k + self.u - lag < TILES

    def tile(self, lag):
        return self.k * 2 + (self.u - lag)

    def slot(self, lag):
        return (self.u - lag) % 2

    def visits(self, lag):
        return self.k + (self.u - lag) // 2

    def count(self, lag, per, more):
        return self.k * (2 * per) + ((self.u - lag) * per + more)


def wait(eng, sem, value):
    if not isinstance(value, int) or value > 0:
        eng.wait_ge(sem, value)


def run_steps(eng, step):
    first = LAST_LAG + LAST_LAG % 2
    for s in range(first):
        step(Step(s // 2, s % 2))
    with eng.Fori(first // 2, TILES // 2) as k:
        step(Step(k, 0))
        step(Step(k, 1))
    for s in range(TILES, STEPS):
        step(Step(s // 2, s % 2))


def build(nc, d, y_out):
    with ExitStack() as ctx:
        def sb(name, shape, dt=F32):
            return ctx.enter_context(nc.sbuf_tensor(name, shape, dt))

        def sem(name):
            return ctx.enter_context(nc.semaphore(name))

        def bank(name):
            return ctx.enter_context(nc.psum_tensor(name, [P, 512], F32))

        ident = sb("ident", [P, P])
        centre = sb("centre", [P, P])
        ws2 = sb("ws2", [P, 2, D_EMB])
        wc2 = sb("wc2", [P, 2 * D_EMB])
        gs_b = sb("gs_b", [P, D_OUT])
        wg_t = sb("wg_t", [P, D_OUT])
        gram = sb("gram", [P, 2 * D_EMB])
        wsi_raw = sb("wsi_raw", [ROWS, GRP * N_PROJ])
        wsi_mask = sb("wsi_mask", [ROWS, GRP * N_PROJ])
        wsi_sum = sb("wsi_sum", [ROWS, 1])
        wsi_mean = sb("wsi_mean", [ROWS, 1])
        wsi = sb("wsi", [ROWS, GRP * N_PROJ])
        ones = sb("ones", [ROWS, PARTS])
        pick = sb("pick", [PARTS, 6])
        bs_b = sb("bs_b", [PARTS, D_OUT])
        s_sum = sb("s_sum", [PARTS, D_OUT])
        part_hi = sb("part_hi", [PARTS, 2, D_OUT], BF16)
        part_mid = sb("part_mid", [PARTS, 2, D_OUT], BF16)
        part_lo = sb("part_lo", [PARTS, 2, D_OUT], BF16)
        rest = sb("rest", [PARTS, 2, D_OUT])
        rest2 = sb("rest2", [PARTS, 2, D_OUT])
        picked = sb("picked", [PARTS, 2, 3, D_OUT])
        bs_rows = sb("bs_rows", [PARTS, D_OUT], BF16)
        s_rows = sb("s_rows", [PARTS, CP, GRP * N_PROJ], BF16)
        wl = sb("wl", [P, QC, D_PAIR])
        wl_sum = sb("wl_sum", [P, QC])
        wl_mean = sb("wl_mean", [P, QC])
        wd = sb("wd", [P, 2, D_OUT])
        wd_sum = sb("wd_sum", [P, 2])
        wd_mean = sb("wd_mean", [P, 2])
        w1 = sb("w1", [P, 5, D_H1])
        w2 = sb("w2", [P, 4, D_H2])
        w3 = sb("w3", [P, 2])
        cols = sb("cols", [P, 14])
        b1, b2 = cols[:, 0:4], cols[:, 4:6]
        gl, bl = cols[:, 6:9], cols[:, 9:12]
        gd, bd = cols[:, 12:13], cols[:, 13:14]
        gsi_b = sb("gsi_b", [P, N_PROJ])
        bsi_b = sb("bsi_b", [P, N_PROJ])
        eps = sb("eps", [P, 1])

        ids = sb("ids", [ROWS, TILES * GROUPS], I32)
        base = sb("base", [ROWS, 1], I32)
        rows = sb("rows", [ROWS, TILES * GROUPS], I32)
        idx = [sb(f"idx{i}", [ROWS, GROUPS], I32) for i in range(2)]
        emb = [sb(f"emb{i}", [ROWS, GROUPS, D_EMB]) for i in range(2)]
        emb_t = sb("emb_t", [P, CHUNKS, CP, ROWS])
        prod = sb("prod", [ROWS, CG, D_EMB])
        q = sb("q", [ROWS, GROUPS])
        q_sd = sb("q_sd", [ROWS, GROUPS])
        q_rstd = sb("q_rstd", [ROWS, GROUPS])
        emb_n = sb("emb_n", [ROWS, GROUPS, D_EMB])
        v = sb("v", [P, CHUNKS, CP * GRP * N_PROJ])
        sq = [sb(f"sq{i}", [P, CP * GRP, N_PROJ]) for i in range(2)]
        ss = sb("ss", [P, CHUNKS, 2, CP * GRP])
        y_sd = sb("y_sd", [P, CHUNKS, 2, CP * GRP])
        y_rstd = sb("y_rstd", [P, CHUNKS, 2, CP * GRP])
        yn = [sb(f"yn{i}", [P, TILE, N_PROJ]) for i in range(2)]
        feat = [sb(f"feat{i}", [P, TILE, 1 + N_PROJ]) for i in range(2)]
        zc = [sb(f"zc{i}", [P, QG, GROUPS, QC]) for i in range(2)]
        zs = [sb(f"zs{i}", [P, GRP, GROUPS, QC]) for i in range(2)]
        dense_x = [sb(f"dense_x{i}", [P, 2, TILE]) for i in range(2)]
        dense_h = [sb(f"dense_h{i}", [P, 2, TILE]) for i in range(2)]
        x_raw = sb("x_raw", [P, D_OUT])
        x_junk = sb("x_junk", [P, D_OUT])
        x_stat = sb("x_stat", [P, 3])
        x_n = sb("x_n", [P, D_OUT])
        o_junk = sb("o_junk", [P, D_PAIR])
        o_stat = sb("o_stat", [P, 3])
        o_n = sb("o_n", [P, D_USED])
        h0 = sb("h0", [P, 3, TILE])
        h1 = sb("h1", [P, 4, TILE])
        h2 = sb("h2", [P, 2, TILE])
        y_all = sb("y_all", [P, TILES])

        pa, pw, pv = bank("pa"), bank("pw"), bank("pv")
        pt = [bank("pt0"), bank("pt1")]
        pz, po, ph = bank("pz"), bank("po"), bank("ph")

        early_loaded, late_loaded, ids_loaded = sem("early_loaded"), sem("late_loaded"), sem("ids_loaded")
        gathered = [[sem(f"gathered{i}_{c}") for c in range(CHUNKS)] for i in range(2)]
        dense_x_loaded = [sem(f"dense_x_loaded{i}") for i in range(2)]
        dense_h_loaded = [sem(f"dense_h_loaded{i}") for i in range(2)]
        zs_loaded = [sem(f"zs_loaded{i}") for i in range(2)]
        out_stored = sem("out_stored")
        rows_ready, idx_ready, chunk_open = sem("rows_ready"), sem("idx_ready"), sem("chunk_open")
        prep_pe, prep_dve = sem("prep_pe"), sem("prep_dve")
        emb_t_done, w_done, v_done, t_done = sem("emb_t_done"), sem("w_done"), sem("v_done"), sem("t_done")
        z_done, o_done, ot_done, x_done = sem("z_done"), sem("o_done"), sem("ot_done"), sem("x_done")
        h1_done, h2_done, xt_done, y_done = sem("h1_done"), sem("h2_done"), sem("xt_done"), sem("y_done")
        emb_t_ready, v_ready, sq_ready, affine_ready = sem("emb_t_ready"), sem("v_ready"), sem("sq_ready"), sem("affine_ready")
        q_sd_ready, y_sd_ready = sem("q_sd_ready"), sem("y_sd_ready")
        x_raw_ready, x_ss_ready, x_sd_ready, x_n_ready, x_ready = (
            sem("x_raw_ready"), sem("x_ss_ready"), sem("x_sd_ready"), sem("x_n_ready"), sem("x_ready"))
        o_ss_ready, o_sd_ready, o_n_ready = sem("o_ss_ready"), sem("o_sd_ready"), sem("o_n_ready")
        h0_ready, h1_ready, h2_ready, y_ready = sem("h0_ready"), sem("h1_ready"), sem("h2_ready"), sem("y_ready")
        prod_ready, q_ready, q_rstd_ready, emb_n_ready = sem("prod_ready"), sem("q_ready"), sem("q_rstd_ready"), sem("emb_n_ready")
        ss_ready, y_rstd_ready, yn_ready = sem("ss_ready"), sem("y_rstd_ready"), sem("yn_ready")
        affine_dve_ready = sem("affine_dve_ready")
        zc_ready, x_rstd_ready, o_rstd_ready = sem("zc_ready"), sem("x_rstd_ready"), sem("o_rstd_ready")

        EARLY = 13
        LATE = 4
        N_PREP = 14

        block = ctx.enter_context(nc.Block())

        @block.sync
        def _(sp):
            sp.dma_start(ids[:], d["ids_t"][:, :]).then_inc(ids_loaded, 16)
            sp.dma_start(base[:], d["table_base"]).then_inc(ids_loaded, 16)
            for to, src in ((ident[:], d["ident"]), (centre[:], d["centre"]), (ws2[:, 0], d["Ws"]), (ws2[:, 1], d["Ws"]),
                            (gs_b[:], d["gs"].to_broadcast([P, D_OUT])), (wsi_raw[:], d["wsi_diag"]),
                            (wsi_mask[:], d["wsi_mask"]), (pick[:], d["pick"]),
                            (bs_b[:], d["bs"].to_broadcast([PARTS, D_OUT])), (cols[:], d["cols"]),
                            (gsi_b[:], d["gsi"].to_broadcast([P, N_PROJ])), (bsi_b[:], d["bsi"].to_broadcast([P, N_PROJ])),
                            (wd[:], d["wd_t"])):
                sp.dma_start(to, src).then_inc(early_loaded, 16)
            for to, src in ((wl[:], d["wl_sq"]), (w1[:], d["w1_k"]), (w2[:], d["w2_k"]), (w3[:], d["w3_k"])):
                sp.dma_start(to, src).then_inc(late_loaded, 16)

            def step(s):
                if s.live(1):
                    wait(sp, x_done, s.count(1, 1, -1))
                    sp.dma_start(dense_x[s.slot(1)][:], d["dense_t"][s.tile(1)]).then_inc(dense_x_loaded[s.slot(1)], 16)
                if s.live(4):
                    wait(sp, h1_done, s.count(4, 1, -1))
                    sp.dma_start(dense_h[s.slot(4)][:], d["dense_t"][s.tile(4)]).then_inc(dense_h_loaded[s.slot(4)], 16)
                if s.live(3):
                    wait(sp, zc_ready, s.count(3, 2, 2))
                    wait(sp, o_done, s.count(3, 1, -1))
                    for c in range(QG):
                        for j in range(GRP):
                            sp.dma_start(zs[s.slot(3)][32 * c:32 * c + 32, j], zc[s.slot(3)][32 * j:32 * j + 32, c]
                                         ).then_inc(zs_loaded[s.slot(3)], 16)

            run_steps(sp, step)
            sp.wait_ge(y_ready, TILES)
            sp.dma_start(y_out, y_all[:]).then_inc(out_stored, 16)
            sp.wait_ge(out_stored, 16)

        @block.gpsimd
        def _(pool):
            pool.wait_ge(ids_loaded, 32)
            nc.gpsimd.tensor_tensor(rows[:], ids[:], base[:].to_broadcast([ROWS, TILES * GROUPS]), ALU.add).then_inc(rows_ready, 1)
            pool.wait_ge(rows_ready, 1)

            def step(s):
                if not s.live(0):
                    return
                for c in range(CHUNKS):
                    wait(pool, gathered[s.slot(0)][c], s.visits(0) * (16 * CG))
                nc.gpsimd.tensor_copy(idx[s.slot(0)][:], rows[:, bass.ds(s.tile(0) * GROUPS, GROUPS)]).then_inc(idx_ready, 1)
                pool.wait_ge(idx_ready, s.count(0, 1, 1))
                for c in range(CHUNKS):
                    wait(pool, emb_n_ready, s.count(0, CHUNKS, c + 1 - 2 * CHUNKS))
                    pool.sem_inc(chunk_open)
                    for g in range(c * CG, (c + 1) * CG):
                        pool.indirect_dma_start(
                            emb[s.slot(0)][:, g], None, d["tables"],
                            bass.IndirectOffsetOnAxis(ap=idx[s.slot(0)][:, g:g + 1], axis=0),
                        ).then_inc(gathered[s.slot(0)][c], 16)

            run_steps(pool, step)

        @block.scalar
        def _(act):
            act.wait_ge(prep_dve, 1)

            def affine(s, projections):
                for p in projections if s.live(2) else ():
                    ins = nc.scalar.activation(feat[s.slot(2)][:, :, 1 + p], yn[s.slot(2)][:, :, p], ACT.Identity,
                                               bias=bsi_b[:, p:p + 1], scale=gsi_b[:, p:p + 1])
                    if p == AFFINE_ACT[-1][-1][-1]:
                        ins.then_inc(affine_ready, 1)

            def step(s):
                for c in range(CHUNKS):
                    if s.live(0):
                        wait(act, emb_t_done, s.count(0, CHUNKS, c + 1))
                        wait(act, w_done, s.count(0, CHUNKS, c + 1 - CHUNKS))
                        nc.scalar.copy(emb_t[:, c].rearrange("p a r -> p (a r)"), pa[:, 0:CP * ROWS]).then_inc(emb_t_ready, 1)
                    if s.live(1):
                        wait(act, v_done, s.count(1, CHUNKS, c + 1))
                        wait(act, t_done, s.count(1, 2 * CHUNKS, 2 * c + 2 - 2 * CHUNKS))
                        nc.scalar.copy(v[:, c], pv[:]).then_inc(v_ready, 1)

                    if s.live(1 if c == 0 else 0):
                        at, b = (1, CHUNKS - 1) if c == 0 else (0, c - 1)
                        wait(act, q_ready, s.count(at, CHUNKS, b + 1))
                        wait(act, q_rstd_ready, s.count(at, CHUNKS, b + 1 - CHUNKS))
                        nc.scalar.activation(q_sd[:, CG * b:CG * (b + 1)], q[:, CG * b:CG * (b + 1)], ACT.Sqrt, bias=eps[:ROWS]).then_inc(q_sd_ready, 1)
                    if s.live(5) and c == 0:
                        wait(act, o_done, s.count(5, 1, 1))
                        wait(act, o_n_ready, s.count(5, 1, 0))
                        nc.scalar.activation(o_junk[:], po[:], ACT.Square, accum_out=o_stat[:, 0:1]).then_inc(o_ss_ready, 1)
                        wait(act, o_ss_ready, s.count(5, 1, 1))
                        nc.scalar.activation(o_stat[:, 1:2], o_stat[:, 0:1], ACT.Sqrt, bias=eps[:], scale=1.0 / D_PAIR).then_inc(o_sd_ready, 1)
                    if s.live(2) and c == 0:
                        if s.fixed and s.tile(2) == 0:
                            act.wait_ge(early_loaded, 16 * EARLY)
                        wait(act, yn_ready, s.count(2, 2 * CHUNKS, 2 * CHUNKS))
                        wait(act, z_done, s.count(2, 2, -2))
                    affine(s, AFFINE_ACT[c][0])
                    if s.live(1):
                        for h in range(2):
                            n = 2 * c + h
                            wait(act, t_done, s.count(1, 2 * CHUNKS, n + 1))
                            wait(act, ss_ready, s.count(1, 2 * CHUNKS, n - 1))
                            nc.scalar.activation(sq[h][:].rearrange("p a b -> p (a b)"), pt[h][:], ACT.Square).then_inc(sq_ready, 1)
                    if s.live(5) and c == 0:
                        wait(act, o_rstd_ready, s.count(5, 1, 1))
                        wait(act, ot_done, s.count(5, 1, 0))
                        nc.scalar.activation(o_n[:], po[:, 0:D_USED], ACT.Copy, scale=o_stat[:, 2:3]).then_inc(o_n_ready, 1)
                    affine(s, AFFINE_ACT[c][1])
                    if s.live(1):
                        wait(act, ss_ready, s.count(1, 2 * CHUNKS, 2 * c + 2))
                        wait(act, y_rstd_ready, s.count(1, CHUNKS, c + 1 - CHUNKS))
                        nc.scalar.activation(y_sd[:, c], ss[:, c], ACT.Sqrt, bias=eps[:], scale=1.0 / N_PROJ).then_inc(y_sd_ready, 1)

                    if c == 0:
                        if s.live(2):
                            wait(act, x_done, s.count(2, 1, 1))
                        if s.live(5):
                            wait(act, ot_done, s.count(5, 1, 1))
                            for k in range(3):
                                last = nc.scalar.activation(h0[:, k], ph[:, P * k:P * (k + 1)], ACT.Identity,
                                                            bias=bl[:, k:k + 1], scale=gl[:, k:k + 1])
                            last.then_inc(h0_ready, 1)
                        if s.live(2):
                            wait(act, x_n_ready, s.count(2, 1, 0))
                            nc.scalar.copy(x_raw[:], ph[:, 384:512]).then_inc(x_raw_ready, 1)
                            wait(act, x_raw_ready, s.count(2, 1, 1))
                            wait(act, x_rstd_ready, s.count(2, 1, 0))
                            nc.scalar.activation(x_junk[:], x_raw[:], ACT.Square, accum_out=x_stat[:, 0:1]).then_inc(x_ss_ready, 1)
                            wait(act, x_ss_ready, s.count(2, 1, 1))
                            nc.scalar.activation(x_stat[:, 1:2], x_stat[:, 0:1], ACT.Sqrt, bias=eps[:], scale=1.0 / D_OUT).then_inc(x_sd_ready, 1)
                    if c == 1 and s.live(2):
                        wait(act, x_rstd_ready, s.count(2, 1, 1))
                        wait(act, xt_done, s.count(2, 1, 0))
                        nc.scalar.activation(x_n[:], x_raw[:], ACT.Copy, scale=x_stat[:, 2:3]).then_inc(x_n_ready, 1)
                    if c == 2:
                        if s.live(2):
                            wait(act, xt_done, s.count(2, 1, 1))
                        if s.live(5):
                            wait(act, h2_done, s.count(5, 1, 1))
                            for m in range(2):
                                last = nc.scalar.activation(h2[:, m], ph[:, P * m:P * (m + 1)], ACT.Relu, bias=b2[:, m:m + 1])
                            last.then_inc(h2_ready, 1)
                        if s.live(2):
                            nc.scalar.activation(feat[s.slot(2)][:].rearrange("p (g j) f -> p j g f", j=GRP)[:, :, :, 0],
                                                 ph[:, 384:512].rearrange("p (j g) -> p j g", j=GRP), ACT.Identity,
                                                 bias=bd, scale=gd).then_inc(x_ready, 1)
            run_steps(act, step)

        @block.vector
        def _(dve):
            links = [0]

            def link(ins):
                links[0] += 1
                ins.then_inc(prep_dve, 1)
                dve.wait_ge(prep_dve, links[0])

            nc.vector.memset(eps[:], EPS)
            nc.vector.memset(ones[:], 1.0)
            link(nc.vector.memset(gram[:], 0.0))
            dve.wait_ge(early_loaded, 16 * EARLY)
            link(nc.vector.reduce_sum(wsi_sum[:], wsi_raw[:], AX))
            link(nc.vector.tensor_scalar(wsi_mean[:], wsi_sum[:], -1.0 / N_PROJ, None, ALU.mult))
            link(nc.vector.scalar_tensor_tensor(wsi[:], wsi_mask[:], wsi_mean[:], wsi_raw[:], ALU.mult, ALU.add))
            dve.wait_ge(prep_pe, 1)
            link(nc.vector.tensor_copy(wc2[:], pa[:, 0:P]))
            dve.wait_ge(prep_pe, 2)
            nc.vector.tensor_tensor(wg_t[:], pw[:, 0:P], gs_b[:], ALU.mult)
            dve.wait_ge(prep_pe, 3)
            for h in range(2):
                rows_h = slice(D_EMB * h, D_EMB * (h + 1))
                nc.vector.tensor_scalar(gram[rows_h, rows_h], pv[rows_h, 0:D_EMB], 1.0 / D_OUT, None, ALU.mult)
            dve.wait_ge(prep_pe, 4)
            nc.vector.tensor_copy(rest[:, 1], bs_b[:])
            link(nc.vector.tensor_copy(rest[:, 0], pz[0:PARTS, 0:P]))
            link(nc.vector.tensor_copy(part_hi[:], rest[:]))
            link(nc.vector.tensor_tensor(rest2[:], rest[:], part_hi[:], ALU.subtract))
            link(nc.vector.tensor_copy(part_mid[:], rest2[:]))
            link(nc.vector.tensor_tensor(rest[:], rest2[:], part_mid[:], ALU.subtract))
            link(nc.vector.tensor_copy(part_lo[:], rest[:]))
            for k in range(2):
                nc.vector.tensor_scalar(picked[:, k, 0], part_hi[:, k], pick[:, 3 * k:3 * k + 1], None, ALU.mult)
            dve.wait_ge(prep_dve, links[0])
            link(nc.vector.tensor_scalar(picked[:, 0, 2], part_lo[:, 0], pick[:, 2:3], None, ALU.mult))
            for k in range(2):
                nc.vector.scalar_tensor_tensor(picked[:, k, 1], part_mid[:, k], pick[:, 3 * k + 1:3 * k + 2], picked[:, k, 0], ALU.mult, ALU.add)
            link(nc.vector.tensor_scalar(picked[:, 1, 2], part_lo[:, 1], pick[:, 5:6], None, ALU.mult))
            nc.vector.tensor_tensor(bs_rows[:], picked[:, 1, 1], picked[:, 1, 2], ALU.add)
            link(nc.vector.tensor_tensor(s_rows[:], picked[:, 0:1, 1].to_broadcast([PARTS, CP, P]),
                                         picked[:, 0:1, 2].to_broadcast([PARTS, CP, P]), ALU.add))
            nc.vector.reduce_sum(wd_sum[:], wd[:], AX)
            dve.wait_ge(late_loaded, 16 * LATE)
            link(nc.vector.reduce_sum(wl_sum[:], wl[:], AX))
            nc.vector.tensor_scalar(wd_mean[:], wd_sum[:], 1.0 / D_OUT, None, ALU.mult)
            link(nc.vector.tensor_scalar(wl_mean[:], wl_sum[:], 1.0 / D_PAIR, None, ALU.mult))
            for k in range(2):
                nc.vector.tensor_scalar(wd[:, k], wd[:, k], wd_mean[:, k:k + 1], None, ALU.subtract)
            for k in range(QC):
                last = nc.vector.tensor_scalar(wl[:, k], wl[:, k], wl_mean[:, k:k + 1], None, ALU.subtract)
            link(last)

            def step(s):
                for c in range(CHUNKS):
                    if s.live(1 if c == 0 else 0):
                        at, b = (1, CHUNKS - 1) if c == 0 else (0, c - 1)
                        g = slice(CG * b, CG * (b + 1))
                        wait(dve, q_sd_ready, s.count(at, CHUNKS, b + 1))
                        nc.vector.reciprocal(q_rstd[:, g], q_sd[:, g]).then_inc(q_rstd_ready, 1)
                        wait(dve, q_rstd_ready, s.count(at, CHUNKS, b + 1))
                        wait(dve, v_done, s.count(at, CHUNKS, b + 1 - CHUNKS))
                        nc.vector.tensor_tensor(emb_n[:, g], emb[s.slot(at)][:, g],
                                                q_rstd[:, g].unsqueeze(2).to_broadcast([ROWS, CG, D_EMB]),
                                                ALU.mult).then_inc(emb_n_ready, 1)
                    if s.live(3) and c % 2:
                        half = c // 2
                        wait(dve, z_done, s.count(3, 2, half + 1))
                        if half == 0:
                            wait(dve, zs_loaded[s.slot(3)], s.visits(3) * (16 * QG * GRP))
                        nc.vector.tensor_copy(zc[s.slot(3)][:, :, 16 * half:16 * (half + 1)],
                                              pz[:].rearrange("p (g c q) -> p c g q", c=QG, q=QC)).then_inc(zc_ready, 1)
                    if s.live(5) and c == 0:
                        wait(dve, o_sd_ready, s.count(5, 1, 1))
                        nc.vector.reciprocal(o_stat[:, 2:3], o_stat[:, 1:2]).then_inc(o_rstd_ready, 1)
                    if s.live(1):
                        for h in range(2):
                            wait(dve, sq_ready, s.count(1, 2 * CHUNKS, 2 * c + h + 1))
                            wait(dve, y_sd_ready, s.count(1, CHUNKS, c + 1 - CHUNKS))
                            nc.vector.reduce_sum(ss[:, c, h], sq[h][:], AX).then_inc(ss_ready, 1)
                    if s.live(2) and c == 1:
                        wait(dve, x_sd_ready, s.count(2, 1, 1))
                        nc.vector.reciprocal(x_stat[:, 2:3], x_stat[:, 1:2]).then_inc(x_rstd_ready, 1)
                    if s.live(0):
                        wait(dve, w_done, s.count(0, CHUNKS, c + 1))
                        nc.vector.tensor_tensor(prod[:], pw[0:ROWS].rearrange("p (a b) -> p a b", b=D_EMB),
                                                emb[s.slot(0)][:, CG * c:CG * (c + 1)], ALU.mult).then_inc(prod_ready, 1)
                    if s.live(1):
                        wait(dve, y_sd_ready, s.count(1, CHUNKS, c + 1))
                        nc.vector.reciprocal(y_rstd[:, c], y_sd[:, c]).then_inc(y_rstd_ready, 1)
                    if s.live(0):
                        wait(dve, prod_ready, s.count(0, CHUNKS, c + 1))
                        wait(dve, q_sd_ready, s.count(0, CHUNKS, c + 1 - CHUNKS))
                        nc.vector.reduce_sum(q[:, CG * c:CG * (c + 1)], prod[:], AX).then_inc(q_ready, 1)
                    if s.live(1):
                        wait(dve, y_rstd_ready, s.count(1, CHUNKS, c + 1))
                        if c == 0:
                            wait(dve, affine_ready, s.count(1, 1, -1))
                        for h in range(2):
                            out = yn[s.slot(1)][:].rearrange("p (a h j) f -> p h a j f", h=2, j=GRP)[:, h, CP * c:CP * (c + 1)]
                            nc.vector.tensor_tensor(
                                out, pt[h][:].rearrange("p (a j f) -> p a j f", a=CP, j=GRP),
                                y_rstd[:, c, h].rearrange("p (a j) -> p a j", a=CP).unsqueeze(3).to_broadcast([P, CP, GRP, N_PROJ]),
                                ALU.mult).then_inc(yn_ready, 1)
                    if s.live(2):
                        if c == 0:
                            wait(dve, yn_ready, s.count(2, 2 * CHUNKS, 2 * CHUNKS))
                            wait(dve, z_done, s.count(2, 2, -2))
                        for p in AFFINE_DVE[c]:
                            last = nc.vector.tensor_scalar(feat[s.slot(2)][:, :, 1 + p], yn[s.slot(2)][:, :, p],
                                                           gsi_b[:, p:p + 1], bsi_b[:, p:p + 1], ALU.mult, ALU.add)
                        if c == CHUNKS - 1:
                            last.then_inc(affine_dve_ready, 1)
                    if c == 1 and s.live(5):
                        wait(dve, h1_done, s.count(5, 1, 1))
                        for m in range(4):
                            last = nc.vector.tensor_scalar(h1[:, m], ph[:, P * m:P * (m + 1)], b1[:, m:m + 1], 0.0, ALU.add, ALU.max)
                        last.then_inc(h1_ready, 1)
                    if c == 3 and s.live(5):
                        wait(dve, y_done, s.count(5, 1, 1))
                        nc.vector.tensor_copy(y_all[:, bass.ds(s.tile(5), 1)], ph[:, 0:1]).then_inc(y_ready, 1)

            run_steps(dve, step)

        @block.tensor
        def _(pe):
            pe.wait_ge(early_loaded, 16 * EARLY)
            ws_flat = ws2[:].rearrange("p h d -> p (h d)")
            nc.tensor.matmul(pa[:, 0:P], centre[:], ws_flat, start=True, stop=True).then_inc(prep_pe, 1)
            nc.tensor.matmul(pw[:, 0:P], ws_flat, centre[:], start=True, stop=True).then_inc(prep_pe, 1)
            pe.wait_ge(prep_dve, 5)
            nc.tensor.matmul(pv[:, 0:D_EMB], wc2[:], wc2[:, 0:D_EMB], start=True, stop=True).then_inc(prep_pe, 1)
            nc.tensor.matmul(pz[0:PARTS, 0:P], ones[:], wsi[:], start=True, stop=True).then_inc(prep_pe, 1)

            def step(s):
                for c in range(CHUNKS):
                    if s.live(0):
                        pe.wait_ge(gathered[s.slot(0)][c], (s.visits(0) + 1) * (16 * CG))
                        wait(pe, emb_t_ready, s.count(0, CHUNKS, c))
                        if s.fixed and s.tile(0) == 0 and c == 0:
                            pe.wait_ge(prep_dve, N_PREP)
                        for a in range(CP):
                            g = CG * c + 2 * a
                            last = nc.tensor.transpose(pa[:, ROWS * a:ROWS * (a + 1)],
                                                       emb[s.slot(0)][:, g:g + 2].rearrange("p g d -> p (g d)"), ident[:ROWS, :ROWS])
                        last.then_inc(emb_t_done, 1)
                    if s.live(1):
                        wait(pe, emb_n_ready, s.count(1, CHUNKS, c + 1))
                        wait(pe, v_ready, s.count(1, CHUNKS, c))
                        for a in range(CP):
                            g = CG * c + 2 * a
                            last = nc.tensor.matmul(pv[:, P * a:P * (a + 1)], emb_n[:, g:g + 2].rearrange("p g d -> p (g d)"), wsi[:],
                                                    start=True, stop=True)
                        last.then_inc(v_done, 1)
                    if s.live(3):
                        if c == 0:
                            wait(pe, affine_ready, s.count(3, 1, 1))
                            wait(pe, affine_dve_ready, s.count(3, 1, 1))
                            wait(pe, x_ready, s.count(3, 1, 1))
                        if c % 2 == 0:
                            wait(pe, zc_ready, s.count(3, 2, c // 2))
                        for g in range(CG * c, CG * (c + 1)):
                            for j in range(GRP):
                                t = feat[s.slot(3)][:, GRP * g + j]
                                col = N_PROJ * (g % 16)
                                last = nc.tensor.matmul(pz[32 * j:32 * j + 32, col:col + N_PROJ], t[:, 1:1 + N_PROJ], t[:, 0:N_PROJ],
                                                        start=True, stop=True)
                        if c % 2:
                            last.then_inc(z_done, 1)
                    if s.live(1):
                        wait(pe, v_ready, s.count(1, CHUNKS, c + 1))
                        for h in range(2):
                            wait(pe, yn_ready, s.count(1, 2 * CHUNKS, 2 * c + h - 1))
                            hd = slice(D_EMB * h, D_EMB * (h + 1))
                            nc.tensor.matmul(pt[h][:], wg_t[hd, :], v[hd, c], start=True, stop=False)
                            nc.tensor.matmul(pt[h][:], bs_rows[:], s_rows[:].rearrange("r a b -> r (a b)"),
                                             start=False, stop=True).then_inc(t_done, 1)
                    if s.live(0):
                        wait(pe, emb_t_ready, s.count(0, CHUNKS, c + 1))
                        wait(pe, prod_ready, s.count(0, CHUNKS, c))
                        for a in range(CP):
                            last = nc.tensor.matmul(pw[0:ROWS, P * a:P * (a + 1)], emb_t[:, c, a], gram[:], start=True, stop=True)
                        last.then_inc(w_done, 1)
                    if s.live(4) and c >= 2:
                        if c == 2:
                            if s.fixed and s.tile(4) == 0:
                                pe.wait_ge(prep_dve, N_PREP + 3)
                            pe.wait_ge(zs_loaded[s.slot(4)], (s.visits(4) + 1) * (16 * QG * GRP))
                            wait(pe, o_n_ready, s.count(4, 1, 0))
                        for k in range(4 * (c - 2), 4 * (c - 2) + 4):
                            last = nc.tensor.matmul(po[:], zs[s.slot(4)][:].rearrange("p j g q -> p (j g) q")[:, :, k], wl[:, k],
                                                    start=(k == 0), stop=(k == QC - 1))
                        if c == 3:
                            last.then_inc(o_done, 1)
                    if c == 0:
                        if s.live(6):
                            wait(pe, y_ready, s.count(6, 1, 1))
                        if s.live(3):
                            wait(pe, x_ready, s.count(3, 1, 1))
                        if s.live(5):
                            wait(pe, o_n_ready, s.count(5, 1, 1))
                            for k in range(3):
                                last = nc.tensor.transpose(ph[:, P * k:P * (k + 1)], o_n[:, P * k:P * (k + 1)], ident[:])
                            last.then_inc(ot_done, 1)
                        if s.live(2):
                            if s.fixed and s.tile(2) == 0:
                                pe.wait_ge(prep_dve, N_PREP + 3)
                            pe.wait_ge(dense_x_loaded[s.slot(2)], (s.visits(2) + 1) * 16)
                            for k in range(2):
                                last = nc.tensor.matmul(ph[:, 384:512], dense_x[s.slot(2)][:, k], wd[:, k], start=(k == 0), stop=(k == 1))
                            last.then_inc(x_done, 1)
                    if c == 1 and s.live(5):
                        if s.fixed and s.tile(5) == 0:
                            pe.wait_ge(late_loaded, 16 * LATE)
                        wait(pe, h0_ready, s.count(5, 1, 1))
                        if s.live(2):
                            wait(pe, x_raw_ready, s.count(2, 1, 1))
                        pe.wait_ge(dense_h_loaded[s.slot(5)], (s.visits(5) + 1) * 16)
                        for m in range(4):
                            for k in range(5):
                                rhs = h0[:, k] if k < 3 else dense_h[s.slot(5)][:, k - 3]
                                last = nc.tensor.matmul(ph[:, P * m:P * (m + 1)], w1[:, k, P * m:P * (m + 1)], rhs, start=(k == 0), stop=(k == 4))
                        last.then_inc(h1_done, 1)
                    if c == 2:
                        if s.live(5):
                            wait(pe, h1_ready, s.count(5, 1, 1))
                            for m in range(2):
                                for k in range(4):
                                    last = nc.tensor.matmul(ph[:, P * m:P * (m + 1)], w2[:, k, P * m:P * (m + 1)], h1[:, k], start=(k == 0), stop=(k == 3))
                            last.then_inc(h2_done, 1)
                        if s.live(2):
                            wait(pe, x_raw_ready, s.count(2, 1, 1))
                            wait(pe, x_n_ready, s.count(2, 1, 1))
                            nc.tensor.transpose(ph[:, 384:512], x_n[:], ident[:]).then_inc(xt_done, 1)
                    if c == 3 and s.live(5):
                        wait(pe, h2_ready, s.count(5, 1, 1))
                        if s.live(2):
                            wait(pe, x_ready, s.count(2, 1, 1))
                        for k in range(2):
                            last = nc.tensor.matmul(ph[:, 0:1], h2[:, k], w3[:, k:k + 1], start=(k == 0), stop=(k == 1))
                        last.then_inc(y_done, 1)

            run_steps(pe, step)


def constants():
    ident = np.eye(P, dtype=np.float32)
    centre = (np.eye(P) - 1.0 / P).astype(np.float32)
    mask = np.kron(np.eye(GRP), np.ones((N_TABLES, N_PROJ))).astype(np.float32)
    pick = np.zeros((PARTS, 6), np.float32)
    for r in range(PARTS):
        pick[r, r // 3] = 1.0
        pick[r, 3 + r % 3] = 1.0
    return ident, centre, mask, pick


def kernel(**inputs):
    import concourse.bacc as bacc
    from concourse.bass_utils import run_bass_kernel_spmd as run

    a = {k: np.asarray(v) for k, v in inputs.items()}
    tables = [a[f"tbl_{i}"] for i in range(N_TABLES)]
    first = np.cumsum([0] + [len(t) for t in tables[:-1]]).astype(np.int32)
    ident, centre, mask, pick = constants()
    wsi_diag = np.zeros((GRP, N_TABLES, GRP, N_PROJ), np.float32)
    for j in range(GRP):
        wsi_diag[j, :, j] = a["L0_rec_Wsi"].T
    wl_sq = np.zeros((QG, N_PROJ, QC, D_PAIR), np.float32)
    pi, pj = np.tril_indices(N_PROJ + 1, k=-1)
    wl_sq[pj // QC, pi - 1, pj % QC] = a["L0_rec_Wl"].T
    w_top1 = np.concatenate([a["W_top1"][:D_USED], a["W_top1"][D_PAIR:]])
    cols = np.concatenate([a["b_top1"].reshape(4, P).T, a["b_top2"].reshape(2, P).T,
                           a["L0_rec_gl"][:D_USED].reshape(3, P).T, a["L0_rec_bl"][:D_USED].reshape(3, P).T,
                           a["L0_rec_gd"][:, None], a["L0_rec_bd"][:, None]], axis=1)
    arrays = {
        "tables": np.concatenate(tables),
        "ids_t": a["ids"].reshape(TILES * GROUPS, ROWS).T,
        "table_base": np.tile(first, GRP)[:, None],
        "ident": ident, "centre": centre, "wsi_mask": mask, "pick": pick,
        "Ws": a["L0_rec_Ws"], "gs": a["L0_rec_gs"][None], "bs": a["L0_rec_bs"][None],
        "wsi_diag": wsi_diag.reshape(ROWS, GRP * N_PROJ),
        "gsi": a["L0_rec_gsi"][None], "bsi": a["L0_rec_bsi"][None], "cols": cols,
        "wd_t": a["L0_rec_Wd"].T.reshape(2, P, D_OUT).transpose(1, 0, 2),
        "wl_sq": wl_sq.reshape(P, QC, D_PAIR),
        "w1_k": w_top1.reshape(5, P, D_H1).transpose(1, 0, 2),
        "w2_k": a["W_top2"].reshape(4, P, D_H2).transpose(1, 0, 2),
        "w3_k": a["W_top3"].reshape(2, P).T,
        "dense_t": a["r_dense_t"].reshape(TILES, GROUPS, GRP, 2, P).transpose(0, 4, 3, 2, 1).reshape(TILES, P, 2, TILE),
    }
    arrays = {k: np.ascontiguousarray(v) for k, v in arrays.items()}
    nc = bacc.Bacc("TRN2", target_bir_lowering=False, num_devices=1)
    d = {k: nc.dram_tensor("in_" + k, v.shape, mybir.dt.from_np(v.dtype), kind="ExternalInput").ap() for k, v in arrays.items()}
    y = nc.dram_tensor("y", (P, TILES), F32, kind="ExternalOutput").ap()
    build(nc, d, y)
    r = run(nc, [{"in_" + k: v for k, v in arrays.items()}], core_ids=[0])
    return r.results[0]["y"].reshape(GRP, GROUPS, TILES).transpose(2, 1, 0).reshape(N_SAMPLES, 1)
```

```python
import numpy as np
import concourse.bass as bass
from concourse import mybir
from contextlib import ExitStack

F32 = mybir.dt.float32
BF16 = mybir.dt.bfloat16
I32 = mybir.dt.int32
ACT = mybir.ActivationFunctionType
ALU = mybir.AluOpType
AX = mybir.AxisListType.X

N_SAMPLES, N_TABLES, D_EMB = 2048, 26, 64
D_DENSE, D_OUT, N_PROJ = 256, 128, 32
D_PAIR, D_USED = 512, 384
D_H1, D_H2 = 512, 256
P = 128
TILE = P
TILES = N_SAMPLES // TILE
GRP = 4
GROUPS = TILE // GRP
ROWS = GRP * N_TABLES
CHUNKS = 4
CG = GROUPS // CHUNKS
CP = CG // 2
MIX_LAG = 2
N_FEAT = N_PROJ + 2
N_COL = N_PROJ + 1
QC = 6
BLOCKS = [(1, 3, 3)] + [(c, QC, min(c + QC - 1, N_PROJ)) for c in range(4, N_COL, QC)]
N_BLOCKS = len(BLOCKS)
ORDER = [N_BLOCKS - 1] + list(range(N_BLOCKS - 1))
PAIR_AT = {b: sum(BLOCKS[o][2] for o in ORDER[:n]) for n, b in enumerate(ORDER)}
PAIR_ROWS = sum(rows for _, _, rows in BLOCKS)
EPS = 1e-5
PARTS = 9
LAST_LAG = 3
STEPS = TILES + LAST_LAG


class Step:

    def __init__(self, k, u):
        self.k, self.u, self.fixed = k, u, isinstance(k, int)

    def live(self, lag):
        return not self.fixed or 0 <= 2 * self.k + self.u - lag < TILES

    def tile(self, lag):
        return self.k * 2 + (self.u - lag)

    def slot(self, lag):
        return (self.u - lag) % 2

    def visits(self, lag):
        return self.k + (self.u - lag) // 2

    def count(self, lag, per, more):
        return self.k * (2 * per) + ((self.u - lag) * per + more)


def mixed(c):
    return (0, c - MIX_LAG) if c >= MIX_LAG else (1, c + CHUNKS - MIX_LAG)


def wait(eng, sem, value):
    if not isinstance(value, int) or value > 0:
        eng.wait_ge(sem, value)


def run_steps(eng, step):
    first = LAST_LAG + LAST_LAG % 2
    for s in range(first):
        step(Step(s // 2, s % 2))
    with eng.Fori(first // 2, TILES // 2) as k:
        step(Step(k, 0))
        step(Step(k, 1))
    for s in range(TILES, STEPS):
        step(Step(s // 2, s % 2))


def build(nc, d, y_out):
    with ExitStack() as ctx:
        def sb(name, shape, dt=F32):
            return ctx.enter_context(nc.sbuf_tensor(name, shape, dt))

        def sem(name):
            return ctx.enter_context(nc.semaphore(name))

        def bank(name):
            return ctx.enter_context(nc.psum_tensor(name, [P, 512], F32))

        ident = sb("ident", [P, P])
        centre = sb("centre", [P, P])
        ws2 = sb("ws2", [P, 2, D_EMB])
        wc2 = sb("wc2", [P, 2 * D_EMB])
        gs_b = sb("gs_b", [P, D_OUT])
        wg_t = sb("wg_t", [P, D_OUT])
        gram = sb("gram", [P, 2 * D_EMB])
        wsi_raw = sb("wsi_raw", [ROWS, GRP * N_PROJ])
        wsi_mask = sb("wsi_mask", [ROWS, GRP * N_PROJ])
        wsi_sum = sb("wsi_sum", [ROWS, 1])
        wsi_mean = sb("wsi_mean", [ROWS, 1])
        wsi = sb("wsi", [ROWS, GRP * N_PROJ])
        ones = sb("ones", [ROWS, PARTS])
        pick = sb("pick", [PARTS, 6])
        bs_b = sb("bs_b", [PARTS, D_OUT])
        s_sum = sb("s_sum", [PARTS, D_OUT])
        part_hi = sb("part_hi", [PARTS, 2, D_OUT], BF16)
        part_mid = sb("part_mid", [PARTS, 2, D_OUT], BF16)
        part_lo = sb("part_lo", [PARTS, 2, D_OUT], BF16)
        rest = sb("rest", [PARTS, 2, D_OUT])
        rest2 = sb("rest2", [PARTS, 2, D_OUT])
        picked = sb("picked", [PARTS, 2, 3, D_OUT])
        bs_rows = sb("bs_rows", [PARTS, D_OUT], BF16)
        s_rows = sb("s_rows", [PARTS, CP, GRP * N_PROJ], BF16)
        wl = sb("wl", [PAIR_ROWS, QC, D_PAIR])
        wl_sum = sb("wl_sum", [PAIR_ROWS, QC])
        wl_mean = sb("wl_mean", [PAIR_ROWS, QC])
        pair_gb = sb("pair_gb", [PAIR_ROWS, 4, QC])
        pair_gg = sb("pair_gg", [PAIR_ROWS, QC])
        pair_coef = sb("pair_coef", [PAIR_ROWS, 3, QC])
        pair_mask = sb("pair_mask", [PAIR_ROWS, 3, QC, N_COL])
        fold_parts = sb("fold_parts", [PAIR_ROWS, 3, QC, N_COL])
        fold_two = sb("fold_two", [PAIR_ROWS, QC, N_COL])
        fold = sb("fold", [PAIR_ROWS, QC, N_COL])
        wd = sb("wd", [P, 2, D_OUT])
        wd_sum = sb("wd_sum", [P, 2])
        wd_mean = sb("wd_mean", [P, 2])
        w1 = sb("w1", [P, 5, D_H1])
        w2 = sb("w2", [P, 4, D_H2])
        w3 = sb("w3", [P, 2])
        cols = sb("cols", [P, 14])
        b1, b2 = cols[:, 0:4], cols[:, 4:6]
        gl, bl = cols[:, 6:9], cols[:, 9:12]
        gd, bd = cols[:, 12:13], cols[:, 13:14]
        eps = sb("eps", [P, 1])

        ids = sb("ids", [ROWS, TILES * GROUPS], I32)
        base = sb("base", [ROWS, 1], I32)
        rows = sb("rows", [ROWS, TILES * GROUPS], I32)
        idx = [sb(f"idx{i}", [ROWS, GROUPS], I32) for i in range(2)]
        emb = [sb(f"emb{i}", [ROWS, GROUPS, D_EMB]) for i in range(2)]
        emb_t = sb("emb_t", [P, CHUNKS, CP, ROWS])
        prod = sb("prod", [ROWS, CG, D_EMB])
        q = sb("q", [ROWS, GROUPS])
        q_sd = sb("q_sd", [ROWS, GROUPS])
        q_rstd = sb("q_rstd", [ROWS, GROUPS])
        emb_n = sb("emb_n", [ROWS, GROUPS, D_EMB])
        v = sb("v", [P, CHUNKS, CP * GRP * N_PROJ])
        sq = [sb(f"sq{i}", [P, CP * GRP, N_PROJ]) for i in range(2)]
        ss = sb("ss", [P, CHUNKS, 2, CP * GRP])
        y_sd = sb("y_sd", [P, CHUNKS, 2, CP * GRP])
        y_rstd = sb("y_rstd", [P, CHUNKS, 2, CP * GRP])
        feat = [sb(f"feat{i}", [P, TILE, N_FEAT]) for i in range(2)]
        zc = [sb(f"zc{i}", [P, N_BLOCKS, GROUPS, QC]) for i in range(2)]
        zs = [sb(f"zs{i}", [PAIR_ROWS, GRP, GROUPS, QC]) for i in range(2)]
        dense_x = [sb(f"dense_x{i}", [P, 2, TILE]) for i in range(2)]
        dense_h = [sb(f"dense_h{i}", [P, 2, TILE]) for i in range(2)]
        x_raw = sb("x_raw", [P, D_OUT])
        x_junk = sb("x_junk", [P, D_OUT])
        x_stat = sb("x_stat", [P, 3])
        x_n = sb("x_n", [P, D_OUT])
        o_junk = sb("o_junk", [P, D_PAIR])
        o_stat = sb("o_stat", [P, 3])
        o_n = sb("o_n", [P, D_USED])
        h0 = sb("h0", [P, 3, TILE])
        h1 = sb("h1", [P, 4, TILE])
        h2 = sb("h2", [P, 2, TILE])
        y_all = sb("y_all", [P, TILES])

        pa, pw, pv = bank("pa"), bank("pw"), bank("pv")
        pt = [bank("pt0"), bank("pt1")]
        pz, po, ph = bank("pz"), bank("po"), bank("ph")

        early_loaded, pairs_loaded, late_loaded = sem("early_loaded"), sem("pairs_loaded"), sem("late_loaded")
        ids_loaded = sem("ids_loaded")
        gathered = [[sem(f"gathered{i}_{c}") for c in range(CHUNKS)] for i in range(2)]
        dense_x_loaded = [sem(f"dense_x_loaded{i}") for i in range(2)]
        dense_h_loaded = [sem(f"dense_h_loaded{i}") for i in range(2)]
        zs_loaded = [sem(f"zs_loaded{i}") for i in range(2)]
        out_stored = sem("out_stored")
        rows_ready, idx_ready, chunk_open = sem("rows_ready"), sem("idx_ready"), sem("chunk_open")
        prep_pe, prep_dve = sem("prep_pe"), sem("prep_dve")
        fold_pe, fold_dve = sem("fold_pe"), sem("fold_dve")
        emb_t_done, w_done, v_done, t_done = sem("emb_t_done"), sem("w_done"), sem("v_done"), sem("t_done")
        z_done, o_done, ot_done, x_done = sem("z_done"), sem("o_done"), sem("ot_done"), sem("x_done")
        h1_done, h2_done, xt_done, y_done = sem("h1_done"), sem("h2_done"), sem("xt_done"), sem("y_done")
        emb_t_ready, v_ready, sq_ready = sem("emb_t_ready"), sem("v_ready"), sem("sq_ready")
        q_sd_ready, y_sd_ready = sem("q_sd_ready"), sem("y_sd_ready")
        x_raw_ready, x_ss_ready, x_sd_ready, x_n_ready, x_ready = (
            sem("x_raw_ready"), sem("x_ss_ready"), sem("x_sd_ready"), sem("x_n_ready"), sem("x_ready"))
        o_ss_ready, o_sd_ready, o_n_ready = sem("o_ss_ready"), sem("o_sd_ready"), sem("o_n_ready")
        h0_ready, h1_ready, h2_ready, y_ready = sem("h0_ready"), sem("h1_ready"), sem("h2_ready"), sem("y_ready")
        prod_ready, q_ready, q_rstd_ready, emb_n_ready = sem("prod_ready"), sem("q_ready"), sem("q_rstd_ready"), sem("emb_n_ready")
        ss_ready, y_rstd_ready, feat_ready = sem("ss_ready"), sem("y_rstd_ready"), sem("feat_ready")
        zc_ready, x_rstd_ready, o_rstd_ready = sem("zc_ready"), sem("x_rstd_ready"), sem("o_rstd_ready")

        EARLY = 11
        PAIRS = 3
        LATE = 3
        N_PREP = 14
        N_FOLD = 8

        block = ctx.enter_context(nc.Block())

        @block.sync
        def _(sp):
            sp.dma_start(ids[:], d["ids_t"][:, :]).then_inc(ids_loaded, 16)
            sp.dma_start(base[:], d["table_base"]).then_inc(ids_loaded, 16)
            for to, src in ((wsi_raw[:], d["wsi_diag"]), (wsi_mask[:], d["wsi_mask"]), (pick[:], d["pick"]),
                            (bs_b[:], d["bs"].to_broadcast([PARTS, D_OUT])), (cols[:], d["cols"])):
                sp.dma_start(to, src).then_inc(early_loaded, 16)
            for to, src in ((wl[:], d["wl_pair"]), (pair_gb[:], d["pair_gb"]), (pair_mask[:], d["pair_mask"])):
                sp.dma_start(to, src).then_inc(pairs_loaded, 16)
            sp.wait_ge(gathered[0][0], 16 * CG)
            for to, src in ((w1[:], d["w1_k"]), (w2[:], d["w2_k"]), (w3[:], d["w3_k"])):
                sp.dma_start(to, src).then_inc(late_loaded, 16)

            def step(s):
                if s.live(1):
                    wait(sp, zc_ready, s.count(1, CHUNKS, CHUNKS))
                    for b, (_, _, n) in enumerate(BLOCKS):
                        for j in range(GRP):
                            sp.dma_start(zs[s.slot(1)][PAIR_AT[b]:PAIR_AT[b] + n, j], zc[s.slot(1)][32 * j:32 * j + n, b]
                                         ).then_inc(zs_loaded[s.slot(1)], 16)

            run_steps(sp, step)
            sp.wait_ge(y_ready, TILES)
            sp.dma_start(y_out, y_all[:]).then_inc(out_stored, 16)
            sp.wait_ge(out_stored, 16)

        @block.gpsimd
        def _(pool):
            pool.wait_ge(ids_loaded, 32)
            nc.gpsimd.tensor_tensor(rows[:], ids[:], base[:].to_broadcast([ROWS, TILES * GROUPS]), ALU.add).then_inc(rows_ready, 1)
            pool.wait_ge(rows_ready, 1)

            def step(s):
                if not s.live(0):
                    return
                for c in range(CHUNKS):
                    wait(pool, gathered[s.slot(0)][c], s.visits(0) * (16 * CG))
                nc.gpsimd.tensor_copy(idx[s.slot(0)][:], rows[:, bass.ds(s.tile(0) * GROUPS, GROUPS)]).then_inc(idx_ready, 1)
                pool.wait_ge(idx_ready, s.count(0, 1, 1))
                for c in range(CHUNKS):
                    wait(pool, emb_n_ready, s.count(0, CHUNKS, c + 1 - 2 * CHUNKS))
                    pool.sem_inc(chunk_open)
                    for g in range(c * CG, (c + 1) * CG):
                        pool.indirect_dma_start(
                            emb[s.slot(0)][:, g], None, d["tables"],
                            bass.IndirectOffsetOnAxis(ap=idx[s.slot(0)][:, g:g + 1], axis=0),
                        ).then_inc(gathered[s.slot(0)][c], 16)

            run_steps(pool, step)

        @block.scalar
        def _(act):
            for to, src in ((ident[:], d["ident"]), (centre[:], d["centre"]), (ws2[:, 0], d["Ws"]), (ws2[:, 1], d["Ws"]),
                            (gs_b[:], d["gs"].to_broadcast([P, D_OUT])), (wd[:], d["wd_t"])):
                act.dma_start(to, src).then_inc(early_loaded, 16)
            act.wait_ge(prep_dve, 1)

            def step(s):
                if s.live(0):
                    wait(act, x_done, s.count(0, 1, -1))
                    act.dma_start(dense_x[s.slot(0)][:], d["dense_t"][s.tile(0)]).then_inc(dense_x_loaded[s.slot(0)], 16)
                if s.live(3):
                    act.dma_start(dense_h[s.slot(3)][:], d["dense_t"][s.tile(3)]).then_inc(dense_h_loaded[s.slot(3)], 16)
                for c in range(CHUNKS):
                    lm, cm = mixed(c)
                    if s.live(0):
                        wait(act, emb_t_done, s.count(0, CHUNKS, c + 1))
                        wait(act, w_done, s.count(0, CHUNKS, c + 1 - CHUNKS))
                        nc.scalar.copy(emb_t[:, c].rearrange("p a r -> p (a r)"), pa[:, 0:CP * ROWS]).then_inc(emb_t_ready, 1)
                    if s.live(lm):
                        wait(act, v_done, s.count(lm, CHUNKS, cm + 1))
                        wait(act, t_done, s.count(lm, 2 * CHUNKS, 2 * cm + 2 - 2 * CHUNKS))
                        nc.scalar.copy(v[:, cm], pv[:]).then_inc(v_ready, 1)
                    if s.live(0) and c == 1:
                        wait(act, x_done, s.count(0, 1, 1))
                        wait(act, x_n_ready, s.count(0, 1, 0))
                        nc.scalar.copy(x_raw[:], ph[:, 384:512]).then_inc(x_raw_ready, 1)
                        wait(act, x_raw_ready, s.count(0, 1, 1))
                        wait(act, x_rstd_ready, s.count(0, 1, 0))
                        nc.scalar.activation(x_junk[:], x_raw[:], ACT.Square, accum_out=x_stat[:, 0:1]).then_inc(x_ss_ready, 1)
                    if s.live(1 if c == 0 else 0):
                        at, b = (1, CHUNKS - 1) if c == 0 else (0, c - 1)
                        wait(act, q_ready, s.count(at, CHUNKS, b + 1))
                        wait(act, q_rstd_ready, s.count(at, CHUNKS, b + 1 - CHUNKS))
                        nc.scalar.activation(q_sd[:, CG * b:CG * (b + 1)], q[:, CG * b:CG * (b + 1)], ACT.Sqrt, bias=eps[:ROWS]).then_inc(q_sd_ready, 1)
                    if s.live(0) and c == 1:
                        wait(act, x_ss_ready, s.count(0, 1, 1))
                        nc.scalar.activation(x_stat[:, 1:2], x_stat[:, 0:1], ACT.Sqrt, bias=eps[:], scale=1.0 / D_OUT).then_inc(x_sd_ready, 1)
                    if s.live(3) and c == 0:
                        wait(act, o_done, s.count(3, 1, 1))
                        wait(act, o_n_ready, s.count(3, 1, 0))
                        nc.scalar.activation(o_junk[:], po[:], ACT.Square, accum_out=o_stat[:, 0:1]).then_inc(o_ss_ready, 1)
                        wait(act, o_ss_ready, s.count(3, 1, 1))
                        nc.scalar.activation(o_stat[:, 1:2], o_stat[:, 0:1], ACT.Sqrt, bias=eps[:], scale=1.0 / D_PAIR).then_inc(o_sd_ready, 1)
                        wait(act, o_rstd_ready, s.count(3, 1, 1))
                        wait(act, ot_done, s.count(3, 1, 0))
                        nc.scalar.activation(o_n[:], po[:, 0:D_USED], ACT.Copy, scale=o_stat[:, 2:3]).then_inc(o_n_ready, 1)
                    if s.live(lm):
                        for h in range(2):
                            n = 2 * cm + h
                            wait(act, t_done, s.count(lm, 2 * CHUNKS, n + 1))
                            wait(act, ss_ready, s.count(lm, 2 * CHUNKS, n - 1))
                            nc.scalar.activation(sq[h][:].rearrange("p a b -> p (a b)"), pt[h][:], ACT.Square).then_inc(sq_ready, 1)
                    if s.live(lm):
                        wait(act, ss_ready, s.count(lm, 2 * CHUNKS, 2 * cm + 2))
                        wait(act, y_rstd_ready, s.count(lm, CHUNKS, cm + 1 - CHUNKS))
                        nc.scalar.activation(y_sd[:, cm], ss[:, cm], ACT.Sqrt, bias=eps[:], scale=1.0 / N_PROJ).then_inc(y_sd_ready, 1)

                    if c == 0:
                        if s.live(0):
                            wait(act, x_done, s.count(0, 1, 1))
                        if s.live(3):
                            wait(act, ot_done, s.count(3, 1, 1))
                            for k in range(3):
                                last = nc.scalar.activation(h0[:, k], ph[:, P * k:P * (k + 1)], ACT.Identity,
                                                            bias=bl[:, k:k + 1], scale=gl[:, k:k + 1])
                            last.then_inc(h0_ready, 1)
                    if c == 1 and s.live(0):
                        wait(act, x_rstd_ready, s.count(0, 1, 1))
                        wait(act, xt_done, s.count(0, 1, 0))
                        nc.scalar.activation(x_n[:], x_raw[:], ACT.Copy, scale=x_stat[:, 2:3]).then_inc(x_n_ready, 1)
                    if c == 2:
                        if s.live(0):
                            wait(act, xt_done, s.count(0, 1, 1))
                        if s.live(3):
                            wait(act, h2_done, s.count(3, 1, 1))
                            for m in range(2):
                                last = nc.scalar.activation(h2[:, m], ph[:, P * m:P * (m + 1)], ACT.Relu, bias=b2[:, m:m + 1])
                            last.then_inc(h2_ready, 1)
                        if s.live(0):
                            if s.fixed and s.tile(0) == 0:
                                act.wait_ge(early_loaded, 16 * EARLY)
                            wait(act, z_done, s.count(0, CHUNKS, -CHUNKS))
                            nc.scalar.activation(feat[s.slot(0)][:].rearrange("p (g j) f -> p j g f", j=GRP)[:, :, :, 0],
                                                 ph[:, 384:512].rearrange("p (j g) -> p j g", j=GRP), ACT.Identity,
                                                 bias=bd, scale=gd).then_inc(x_ready, 1)
            run_steps(act, step)

        @block.vector
        def _(dve):
            links = [0]

            def link(ins):
                links[0] += 1
                ins.then_inc(prep_dve, 1)
                dve.wait_ge(prep_dve, links[0])

            nc.vector.memset(eps[:], EPS)
            nc.vector.memset(ones[:], 1.0)
            link(nc.vector.memset(gram[:], 0.0))
            dve.wait_ge(early_loaded, 16 * EARLY)
            link(nc.vector.reduce_sum(wsi_sum[:], wsi_raw[:], AX))
            link(nc.vector.tensor_scalar(wsi_mean[:], wsi_sum[:], -1.0 / N_PROJ, None, ALU.mult))
            link(nc.vector.scalar_tensor_tensor(wsi[:], wsi_mask[:], wsi_mean[:], wsi_raw[:], ALU.mult, ALU.add))
            dve.wait_ge(prep_pe, 1)
            link(nc.vector.tensor_copy(wc2[:], pa[:, 0:P]))
            dve.wait_ge(prep_pe, 2)
            nc.vector.tensor_tensor(wg_t[:], pw[:, 0:P], gs_b[:], ALU.mult)
            dve.wait_ge(prep_pe, 3)
            for h in range(2):
                rows_h = slice(D_EMB * h, D_EMB * (h + 1))
                nc.vector.tensor_scalar(gram[rows_h, rows_h], pv[rows_h, 0:D_EMB], 1.0 / D_OUT, None, ALU.mult)
            dve.wait_ge(prep_pe, 4)
            nc.vector.tensor_copy(rest[:, 1], bs_b[:])
            link(nc.vector.tensor_copy(rest[:, 0], pz[0:PARTS, 0:P]))
            link(nc.vector.tensor_copy(part_hi[:], rest[:]))
            link(nc.vector.tensor_tensor(rest2[:], rest[:], part_hi[:], ALU.subtract))
            link(nc.vector.tensor_copy(part_mid[:], rest2[:]))
            link(nc.vector.tensor_tensor(rest[:], rest2[:], part_mid[:], ALU.subtract))
            link(nc.vector.tensor_copy(part_lo[:], rest[:]))
            for k in range(2):
                nc.vector.tensor_scalar(picked[:, k, 0], part_hi[:, k], pick[:, 3 * k:3 * k + 1], None, ALU.mult)
            dve.wait_ge(prep_dve, links[0])
            link(nc.vector.tensor_scalar(picked[:, 0, 2], part_lo[:, 0], pick[:, 2:3], None, ALU.mult))
            for k in range(2):
                nc.vector.scalar_tensor_tensor(picked[:, k, 1], part_mid[:, k], pick[:, 3 * k + 1:3 * k + 2], picked[:, k, 0], ALU.mult, ALU.add)
            link(nc.vector.tensor_scalar(picked[:, 1, 2], part_lo[:, 1], pick[:, 5:6], None, ALU.mult))
            nc.vector.tensor_tensor(bs_rows[:], picked[:, 1, 1], picked[:, 1, 2], ALU.add)
            link(nc.vector.tensor_tensor(s_rows[:], picked[:, 0:1, 1].to_broadcast([PARTS, CP, P]),
                                         picked[:, 0:1, 2].to_broadcast([PARTS, CP, P]), ALU.add))
            link(nc.vector.reduce_sum(wd_sum[:], wd[:], AX))
            link(nc.vector.tensor_scalar(wd_mean[:], wd_sum[:], 1.0 / D_OUT, None, ALU.mult))
            for k in range(2):
                last = nc.vector.tensor_scalar(wd[:, k], wd[:, k], wd_mean[:, k:k + 1], None, ALU.subtract)
            link(last)
            for i in range(2):
                nc.vector.memset(feat[i][:, :, N_PROJ + 1:N_FEAT], 1.0)
                nc.vector.memset(zc[i][:, 0, :, BLOCKS[0][1]:QC], 1.0)

            folds = [0]

            def fold_link(ins):
                folds[0] += 1
                ins.then_inc(fold_dve, 1)
                dve.wait_ge(fold_dve, folds[0])

            def centre_pairs():
                dve.wait_ge(pairs_loaded, 16 * PAIRS)
                g_row, b_row, g_col, b_col = (pair_gb[:, k] for k in range(4))
                nc.vector.tensor_tensor(pair_gg[:], g_row, g_col, ALU.mult)
                nc.vector.tensor_tensor(pair_coef[:, 0], b_col, g_row, ALU.mult)
                nc.vector.tensor_tensor(pair_coef[:, 1], b_row, g_col, ALU.mult)
                fold_link(nc.vector.tensor_tensor(pair_coef[:, 2], b_row, b_col, ALU.mult))
                fold_link(nc.vector.tensor_tensor(fold_parts[:], pair_mask[:],
                                             pair_coef[:].unsqueeze(3).to_broadcast([PAIR_ROWS, 3, QC, N_COL]), ALU.mult))
                fold_link(nc.vector.tensor_tensor(fold_two[:], fold_parts[:, 0], fold_parts[:, 1], ALU.add))
                nc.vector.tensor_tensor(fold[:], fold_two[:], fold_parts[:, 2], ALU.add)
                fold_link(nc.vector.reduce_sum(wl_sum[:], wl[:], AX))
                fold_link(nc.vector.tensor_scalar(wl_mean[:], wl_sum[:], 1.0 / D_PAIR, None, ALU.mult))
                for k in range(QC):
                    last = nc.vector.tensor_scalar(wl[:, k], wl[:, k], wl_mean[:, k:k + 1], None, ALU.subtract)
                fold_link(last)

            def scale_pairs():
                dve.wait_ge(fold_pe, 1)
                for k in range(QC):
                    last = nc.vector.tensor_scalar(wl[:, k], wl[:, k], pair_gg[:, k:k + 1], None, ALU.mult)
                fold_link(last)
                fold_link(nc.vector.tensor_copy(wl[0:N_COL, QC - 1], po[0:N_COL]))

            def step(s):
                for c in range(CHUNKS):
                    lm, cm = mixed(c)
                    if s.live(1 if c == 0 else 0):
                        at, b = (1, CHUNKS - 1) if c == 0 else (0, c - 1)
                        g = slice(CG * b, CG * (b + 1))
                        wait(dve, q_sd_ready, s.count(at, CHUNKS, b + 1))
                        nc.vector.reciprocal(q_rstd[:, g], q_sd[:, g]).then_inc(q_rstd_ready, 1)
                        wait(dve, q_rstd_ready, s.count(at, CHUNKS, b + 1))
                        wait(dve, v_done, s.count(at, CHUNKS, b + 1 - CHUNKS))
                        nc.vector.tensor_tensor(emb_n[:, g], emb[s.slot(at)][:, g],
                                                q_rstd[:, g].unsqueeze(2).to_broadcast([ROWS, CG, D_EMB]),
                                                ALU.mult).then_inc(emb_n_ready, 1)
                    if s.live(3) and c == 0:
                        wait(dve, o_sd_ready, s.count(3, 1, 1))
                        nc.vector.reciprocal(o_stat[:, 2:3], o_stat[:, 1:2]).then_inc(o_rstd_ready, 1)
                    if s.live(1):
                        wait(dve, z_done, s.count(1, CHUNKS, c + 1))
                        if c == 0:
                            wait(dve, zs_loaded[s.slot(1)], s.visits(1) * (16 * N_BLOCKS * GRP))
                        dots = pz[:, 0:CG * N_COL].rearrange("p (g c) -> p g c", c=N_COL)
                        first = BLOCKS[0][1]
                        nc.vector.tensor_copy(zc[s.slot(1)][:, 0, CG * c:CG * (c + 1), 0:first], dots[:, :, 0:first])
                        nc.vector.tensor_copy(zc[s.slot(1)][:, 1:, CG * c:CG * (c + 1)],
                                              dots[:, :, first:].rearrange("p g (b q) -> p b g q", q=QC)).then_inc(zc_ready, 1)
                    if s.live(lm):
                        for h in range(2):
                            wait(dve, sq_ready, s.count(lm, 2 * CHUNKS, 2 * cm + h + 1))
                            wait(dve, y_sd_ready, s.count(lm, CHUNKS, cm + 1 - CHUNKS))
                            nc.vector.reduce_sum(ss[:, cm, h], sq[h][:], AX).then_inc(ss_ready, 1)
                    if s.live(0) and c == 1:
                        wait(dve, x_sd_ready, s.count(0, 1, 1))
                        nc.vector.reciprocal(x_stat[:, 2:3], x_stat[:, 1:2]).then_inc(x_rstd_ready, 1)
                    if s.live(0):
                        wait(dve, w_done, s.count(0, CHUNKS, c + 1))
                        nc.vector.tensor_tensor(prod[:], pw[0:ROWS].rearrange("p (a b) -> p a b", b=D_EMB),
                                                emb[s.slot(0)][:, CG * c:CG * (c + 1)], ALU.mult).then_inc(prod_ready, 1)
                    if s.live(lm):
                        wait(dve, y_sd_ready, s.count(lm, CHUNKS, cm + 1))
                        nc.vector.reciprocal(y_rstd[:, cm], y_sd[:, cm]).then_inc(y_rstd_ready, 1)
                    if s.live(0):
                        wait(dve, prod_ready, s.count(0, CHUNKS, c + 1))
                        wait(dve, q_sd_ready, s.count(0, CHUNKS, c + 1 - CHUNKS))
                        nc.vector.reduce_sum(q[:, CG * c:CG * (c + 1)], prod[:], AX).then_inc(q_ready, 1)
                    if s.live(lm):
                        wait(dve, y_rstd_ready, s.count(lm, CHUNKS, cm + 1))
                        if cm == 0:
                            wait(dve, z_done, s.count(lm, CHUNKS, -CHUNKS))
                        for h in range(2):
                            out = feat[s.slot(lm)][:].rearrange("p (a h j) f -> p h a j f", h=2, j=GRP)[:, h, CP * cm:CP * (cm + 1), :, 1:1 + N_PROJ]
                            nc.vector.tensor_tensor(
                                out, pt[h][:].rearrange("p (a j f) -> p a j f", a=CP, j=GRP),
                                y_rstd[:, cm, h].rearrange("p (a j) -> p a j", a=CP).unsqueeze(3).to_broadcast([P, CP, GRP, N_PROJ]),
                                ALU.mult).then_inc(feat_ready, 1)
                    if c == 1 and s.live(3):
                        wait(dve, h1_done, s.count(3, 1, 1))
                        for m in range(4):
                            last = nc.vector.tensor_scalar(h1[:, m], ph[:, P * m:P * (m + 1)], b1[:, m:m + 1], 0.0, ALU.add, ALU.max)
                        last.then_inc(h1_ready, 1)
                    if c == 3 and s.live(3):
                        wait(dve, y_done, s.count(3, 1, 1))
                        nc.vector.tensor_copy(y_all[:, bass.ds(s.tile(3), 1)], ph[:, 0:1]).then_inc(y_ready, 1)
                    if s.fixed and s.live(0) and s.tile(0) == 0 and c == 0:
                        centre_pairs()
                    if s.fixed and s.live(0) and s.tile(0) == 0 and c == 2:
                        scale_pairs()

            run_steps(dve, step)

        @block.tensor
        def _(pe):
            pe.wait_ge(early_loaded, 16 * EARLY)
            ws_flat = ws2[:].rearrange("p h d -> p (h d)")
            nc.tensor.matmul(pa[:, 0:P], centre[:], ws_flat, start=True, stop=True).then_inc(prep_pe, 1)
            nc.tensor.matmul(pw[:, 0:P], ws_flat, centre[:], start=True, stop=True).then_inc(prep_pe, 1)
            pe.wait_ge(prep_dve, 5)
            nc.tensor.matmul(pv[:, 0:D_EMB], wc2[:], wc2[:, 0:D_EMB], start=True, stop=True).then_inc(prep_pe, 1)
            nc.tensor.matmul(pz[0:PARTS, 0:P], ones[:], wsi[:], start=True, stop=True).then_inc(prep_pe, 1)

            PROJECT = {2: range(0, 2), 3: range(2, QC)}

            def step(s):
                for c in range(CHUNKS):
                    lm, cm = mixed(c)
                    if s.live(0):
                        pe.wait_ge(gathered[s.slot(0)][c], (s.visits(0) + 1) * (16 * CG))
                        wait(pe, emb_t_ready, s.count(0, CHUNKS, c))
                        for a in range(CP):
                            g = CG * c + 2 * a
                            last = nc.tensor.transpose(pa[:, ROWS * a:ROWS * (a + 1)],
                                                       emb[s.slot(0)][:, g:g + 2].rearrange("p g d -> p (g d)"), ident[:ROWS, :ROWS])
                        last.then_inc(emb_t_done, 1)
                    if s.live(lm):
                        wait(pe, emb_n_ready, s.count(lm, CHUNKS, cm + 1))
                        wait(pe, v_ready, s.count(lm, CHUNKS, cm))
                        for a in range(CP):
                            g = CG * cm + 2 * a
                            last = nc.tensor.matmul(pv[:, P * a:P * (a + 1)], emb_n[:, g:g + 2].rearrange("p g d -> p (g d)"), wsi[:],
                                                    start=True, stop=True)
                        last.then_inc(v_done, 1)
                    if s.live(1):
                        wait(pe, feat_ready, s.count(1, 2 * CHUNKS, 2 * c + 2))
                        if c == 0:
                            wait(pe, x_ready, s.count(1, 1, 1))
                        wait(pe, zc_ready, s.count(1, CHUNKS, c))
                        for g in range(CG):
                            for j in range(GRP):
                                t = feat[s.slot(1)][:, GRP * (CG * c + g) + j]
                                last = nc.tensor.matmul(pz[32 * j:32 * j + 32, N_COL * g:N_COL * (g + 1)], t[:, 0:N_PROJ], t[:, 1:N_FEAT],
                                                        start=True, stop=True)
                        last.then_inc(z_done, 1)
                    if s.live(lm):
                        if s.fixed and s.tile(lm) == 0 and cm == 0:
                            pe.wait_ge(prep_dve, N_PREP)
                        wait(pe, v_ready, s.count(lm, CHUNKS, cm + 1))
                        for h in range(2):
                            wait(pe, feat_ready, s.count(lm, 2 * CHUNKS, 2 * cm + h - 1))
                            hd = slice(D_EMB * h, D_EMB * (h + 1))
                            nc.tensor.matmul(pt[h][:], wg_t[hd, :], v[hd, cm], start=True, stop=False)
                            nc.tensor.matmul(pt[h][:], bs_rows[:], s_rows[:].rearrange("r a b -> r (a b)"),
                                             start=False, stop=True).then_inc(t_done, 1)
                    if s.live(0):
                        if s.fixed and s.tile(0) == 0 and c == 0:
                            pe.wait_ge(prep_dve, 6)
                        wait(pe, emb_t_ready, s.count(0, CHUNKS, c + 1))
                        wait(pe, prod_ready, s.count(0, CHUNKS, c))
                        for a in range(CP):
                            last = nc.tensor.matmul(pw[0:ROWS, P * a:P * (a + 1)], emb_t[:, c, a], gram[:], start=True, stop=True)
                        last.then_inc(w_done, 1)
                    if s.fixed and s.live(0) and s.tile(0) == 0 and c == 1:
                        pe.wait_ge(fold_dve, 6)
                        for k in range(QC):
                            last = nc.tensor.matmul(po[0:N_COL], fold[:, k], wl[:, k], start=(k == 0), stop=(k == QC - 1))
                        last.then_inc(fold_pe, 1)
                    if s.live(2) and c >= 2:
                        if c == 2:
                            if s.fixed and s.tile(2) == 0:
                                pe.wait_ge(fold_dve, N_FOLD)
                            pe.wait_ge(zs_loaded[s.slot(2)], (s.visits(2) + 1) * (16 * N_BLOCKS * GRP))
                            wait(pe, o_n_ready, s.count(2, 1, 0))
                        for k in PROJECT[c]:
                            last = nc.tensor.matmul(po[:], zs[s.slot(2)][:].rearrange("p j g q -> p (j g) q")[:, :, k], wl[:, k],
                                                    start=(k == 0), stop=(k == QC - 1))
                        if c == 3:
                            last.then_inc(o_done, 1)
                    if c == 0:
                        if s.live(4):
                            wait(pe, y_ready, s.count(4, 1, 1))
                        if s.live(1):
                            wait(pe, x_ready, s.count(1, 1, 1))
                        if s.live(3):
                            wait(pe, o_n_ready, s.count(3, 1, 1))
                            for k in range(3):
                                last = nc.tensor.transpose(ph[:, P * k:P * (k + 1)], o_n[:, P * k:P * (k + 1)], ident[:])
                            last.then_inc(ot_done, 1)
                        if s.live(0):
                            if s.fixed and s.tile(0) == 0:
                                pe.wait_ge(prep_dve, N_PREP + 3)
                            pe.wait_ge(dense_x_loaded[s.slot(0)], (s.visits(0) + 1) * 16)
                            for k in range(2):
                                last = nc.tensor.matmul(ph[:, 384:512], dense_x[s.slot(0)][:, k], wd[:, k], start=(k == 0), stop=(k == 1))
                            last.then_inc(x_done, 1)
                    if c == 1 and s.live(3):
                        if s.fixed and s.tile(3) == 0:
                            pe.wait_ge(late_loaded, 16 * LATE)
                        wait(pe, h0_ready, s.count(3, 1, 1))
                        if s.live(0):
                            wait(pe, x_raw_ready, s.count(0, 1, 1))
                        pe.wait_ge(dense_h_loaded[s.slot(3)], (s.visits(3) + 1) * 16)
                        for m in range(4):
                            for k in range(5):
                                rhs = h0[:, k] if k < 3 else dense_h[s.slot(3)][:, k - 3]
                                last = nc.tensor.matmul(ph[:, P * m:P * (m + 1)], w1[:, k, P * m:P * (m + 1)], rhs, start=(k == 0), stop=(k == 4))
                        last.then_inc(h1_done, 1)
                    if c == 2:
                        if s.live(3):
                            wait(pe, h1_ready, s.count(3, 1, 1))
                            for m in range(2):
                                for k in range(4):
                                    last = nc.tensor.matmul(ph[:, P * m:P * (m + 1)], w2[:, k, P * m:P * (m + 1)], h1[:, k], start=(k == 0), stop=(k == 3))
                            last.then_inc(h2_done, 1)
                        if s.live(0):
                            wait(pe, x_raw_ready, s.count(0, 1, 1))
                            wait(pe, x_n_ready, s.count(0, 1, 1))
                            nc.tensor.transpose(ph[:, 384:512], x_n[:], ident[:]).then_inc(xt_done, 1)
                    if c == 3 and s.live(3):
                        wait(pe, h2_ready, s.count(3, 1, 1))
                        if s.live(0):
                            wait(pe, x_ready, s.count(0, 1, 1))
                        for k in range(2):
                            last = nc.tensor.matmul(ph[:, 0:1], h2[:, k], w3[:, k:k + 1], start=(k == 0), stop=(k == 1))
                        last.then_inc(y_done, 1)

            run_steps(pe, step)


def constants():
    ident = np.eye(P, dtype=np.float32)
    centre = (np.eye(P) - 1.0 / P).astype(np.float32)
    mask = np.kron(np.eye(GRP), np.ones((N_TABLES, N_PROJ))).astype(np.float32)
    pick = np.zeros((PARTS, 6), np.float32)
    for r in range(PARTS):
        pick[r, r // 3] = 1.0
        pick[r, 3 + r % 3] = 1.0
    return ident, centre, mask, pick


def pair_layout():
    row = np.zeros(PAIR_ROWS, int)
    col = np.full((PAIR_ROWS, QC), N_COL)
    for b, (first, n_cols, n_rows) in enumerate(BLOCKS):
        at = slice(PAIR_AT[b], PAIR_AT[b] + n_rows)
        row[at] = np.arange(n_rows)
        col[at, :n_cols] = first + np.arange(n_cols)
    return row, col


def pair_mask(row, col):
    mask = np.zeros((PAIR_ROWS, 3, QC, N_COL), np.float32)
    r = np.arange(N_PROJ)
    mask[:, 0, :, :N_PROJ] = row[:, None, None] == r
    mask[:, 1, :, :N_PROJ] = col[:, :, None] == r
    mask[:, 1, :, 1:N_PROJ] -= (col == N_PROJ)[:, :, None]
    mask[:, 2, :, N_PROJ] = D_OUT
    return mask


def kernel(**inputs):
    import concourse.bacc as bacc
    from concourse.bass_utils import run_bass_kernel_spmd as run

    a = {k: np.asarray(v) for k, v in inputs.items()}
    tables = [a[f"tbl_{i}"] for i in range(N_TABLES)]
    first = np.cumsum([0] + [len(t) for t in tables[:-1]]).astype(np.int32)
    ident, centre, mask, pick = constants()
    wsi_diag = np.zeros((GRP, N_TABLES, GRP, N_PROJ), np.float32)
    for j in range(GRP):
        wsi_diag[j, :, j] = a["L0_rec_Wsi"].T
    pi, pj = np.tril_indices(N_PROJ + 1, k=-1)
    wl_full = np.zeros((N_PROJ + 1, N_COL + 1, D_PAIR), np.float32)
    wl_full[pj, pi] = a["L0_rec_Wl"].T
    row, col = pair_layout()
    wl_pair = wl_full[row[:, None], col]
    g_feat = np.concatenate([np.ones(1, np.float32), a["L0_rec_gsi"], np.ones(1, np.float32)])
    b_feat = np.concatenate([np.zeros(1, np.float32), a["L0_rec_bsi"], np.zeros(1, np.float32)])
    row_all = np.tile(row[:, None], (1, QC))
    pair_gb = np.stack([g_feat[row_all], b_feat[row_all], g_feat[col], b_feat[col]], axis=1)
    w_top1 = np.concatenate([a["W_top1"][:D_USED], a["W_top1"][D_PAIR:]])
    cols = np.concatenate([a["b_top1"].reshape(4, P).T, a["b_top2"].reshape(2, P).T,
                           a["L0_rec_gl"][:D_USED].reshape(3, P).T, a["L0_rec_bl"][:D_USED].reshape(3, P).T,
                           a["L0_rec_gd"][:, None], a["L0_rec_bd"][:, None]], axis=1)
    arrays = {
        "tables": np.concatenate(tables),
        "ids_t": a["ids"].reshape(TILES * GROUPS, ROWS).T,
        "table_base": np.tile(first, GRP)[:, None],
        "ident": ident, "centre": centre, "wsi_mask": mask, "pick": pick,
        "Ws": a["L0_rec_Ws"], "gs": a["L0_rec_gs"][None], "bs": a["L0_rec_bs"][None],
        "wsi_diag": wsi_diag.reshape(ROWS, GRP * N_PROJ),
        "cols": cols, "pair_gb": pair_gb, "pair_mask": pair_mask(row, col), "wl_pair": wl_pair,
        "wd_t": a["L0_rec_Wd"].T.reshape(2, P, D_OUT).transpose(1, 0, 2),
        "w1_k": w_top1.reshape(5, P, D_H1).transpose(1, 0, 2),
        "w2_k": a["W_top2"].reshape(4, P, D_H2).transpose(1, 0, 2),
        "w3_k": a["W_top3"].reshape(2, P).T,
        "dense_t": a["r_dense_t"].reshape(TILES, GROUPS, GRP, 2, P).transpose(0, 4, 3, 2, 1).reshape(TILES, P, 2, TILE),
    }
    arrays = {k: np.ascontiguousarray(v) for k, v in arrays.items()}
    nc = bacc.Bacc("TRN2", target_bir_lowering=False, num_devices=1)
    d = {k: nc.dram_tensor("in_" + k, v.shape, mybir.dt.from_np(v.dtype), kind="ExternalInput").ap() for k, v in arrays.items()}
    y = nc.dram_tensor("y", (P, TILES), F32, kind="ExternalOutput").ap()
    build(nc, d, y)
    r = run(nc, [{"in_" + k: v for k, v in arrays.items()}], core_ids=[0])
    return r.results[0]["y"].reshape(GRP, GROUPS, TILES).transpose(2, 1, 0).reshape(N_SAMPLES, 1)
```

```python
import numpy as np
import concourse.bass as bass
from concourse import mybir
from contextlib import ExitStack

F32 = mybir.dt.float32
I32 = mybir.dt.int32
ACT = mybir.ActivationFunctionType
ALU = mybir.AluOpType
AX = mybir.AxisListType.X

N_SAMPLES, N_TABLES, D_EMB = 2048, 26, 64
D_DENSE, D_OUT, N_PROJ = 256, 128, 32
D_PAIR, D_USED = 512, 384
D_H1, D_H2 = 512, 256
P = 128
TILE = P
TILES = N_SAMPLES // TILE
GRP = 4
GROUPS = TILE // GRP
HALF = TILE // 2
KT = HALF * N_TABLES // P
TOUCH = max((P * k + P - 1) // N_TABLES - P * k // N_TABLES + 1 for k in range(KT))
CHUNKS = 4
CG = GROUPS // CHUNKS
CS = HALF // CHUNKS
K_END = [-(-CS * N_TABLES * (c + 1) // P) for c in range(CHUNKS)]
K_OF = [range(K_END[c - 1] if c else 0, K_END[c]) for c in range(CHUNKS)]
GATHERS = 2 * KT
MIX_LAG = 2
N_FEAT = N_PROJ + 2
N_COL = N_PROJ + 1
QC = 5
BLOCKS = [(1, 3, 3)] + [(c, QC, min(c + QC - 1, N_PROJ)) for c in range(4, N_COL, QC)]
N_BLOCKS = len(BLOCKS)
ORDER = [N_BLOCKS - 1] + list(range(N_BLOCKS - 1))
PAIR_AT = {b: sum(BLOCKS[o][2] for o in ORDER[:n]) for n, b in enumerate(ORDER)}
PAIR_ROWS = sum(rows for _, _, rows in BLOCKS)
EPS = 1e-5
LAST_LAG = 3
STEPS = TILES + LAST_LAG


def gathers_of(c):
    return slice(2 * K_OF[c][0], 2 * K_OF[c][-1] + 2)


def mix_places(c):
    places = []
    for k in range(KT):
        first, last = P * k // N_TABLES, (P * k + P - 1) // N_TABLES
        lo, hi = max(first, CS * c), min(last, CS * (c + 1) - 1)
        if lo <= hi:
            places.append((k, lo - first, lo - CS * c, hi - lo + 1))
    return places


class Step:

    def __init__(self, k, u):
        self.k, self.u, self.fixed = k, u, isinstance(k, int)

    def live(self, lag):
        return not self.fixed or 0 <= 2 * self.k + self.u - lag < TILES

    def tile(self, lag):
        return self.k * 2 + (self.u - lag)

    def slot(self, lag):
        return (self.u - lag) % 2

    def visits(self, lag):
        return self.k + (self.u - lag) // 2

    def count(self, lag, per, more):
        return self.k * (2 * per) + ((self.u - lag) * per + more)


def mixed(c):
    return (0, c - MIX_LAG) if c >= MIX_LAG else (1, c + CHUNKS - MIX_LAG)


def wait(eng, sem, value):
    if not isinstance(value, int) or value > 0:
        eng.wait_ge(sem, value)


def run_steps(eng, step):
    first = LAST_LAG + LAST_LAG % 2
    for s in range(first):
        step(Step(s // 2, s % 2))
    with eng.Fori(first // 2, TILES // 2) as k:
        step(Step(k, 0))
        step(Step(k, 1))
    for s in range(TILES, STEPS):
        step(Step(s // 2, s % 2))


def build(nc, d, dots, y_out):
    with ExitStack() as ctx:
        def sb(name, shape, dt=F32):
            return ctx.enter_context(nc.sbuf_tensor(name, shape, dt))

        def sem(name):
            return ctx.enter_context(nc.semaphore(name))

        def bank(name):
            return ctx.enter_context(nc.psum_tensor(name, [P, 512], F32))

        ident = sb("ident", [P, P])
        centre = sb("centre", [P, P])
        ws2 = sb("ws2", [P, 2, D_EMB])
        wc2 = sb("wc2", [P, 2 * D_EMB])
        gs_b = sb("gs_b", [P, D_OUT])
        wg_t = sb("wg_t", [P, D_OUT])
        gram = sb("gram", [P, 2 * D_EMB])
        wsi_raw = sb("wsi_raw", [P, KT, N_PROJ])
        wsi_mask = sb("wsi_mask", [P, KT, TOUCH])
        wsi_sum = sb("wsi_sum", [P, KT])
        wsi_mean = sb("wsi_mean", [P, KT])
        wsi_c = sb("wsi_c", [P, KT, N_PROJ])
        wsi = sb("wsi", [P, KT, TOUCH, N_PROJ])
        ones = sb("ones", [N_TABLES, P])
        y_bias = sb("y_bias", [P, N_PROJ])
        wl = sb("wl", [PAIR_ROWS, QC, D_PAIR])
        wl_junk = sb("wl_junk", [PAIR_ROWS, QC, D_PAIR])
        wl_sum = sb("wl_sum", [PAIR_ROWS, QC])
        wl_mean = sb("wl_mean", [PAIR_ROWS, QC])
        pair_gb = sb("pair_gb", [PAIR_ROWS, 4, QC])
        pair_gg = sb("pair_gg", [PAIR_ROWS, QC])
        pair_coef = sb("pair_coef", [PAIR_ROWS, 3, QC])
        pair_mask = sb("pair_mask", [PAIR_ROWS, 3, QC, N_COL])
        fold_parts = sb("fold_parts", [PAIR_ROWS, 3, QC, N_COL])
        fold_two = sb("fold_two", [PAIR_ROWS, QC, N_COL])
        fold = sb("fold", [PAIR_ROWS, QC, N_COL])
        wd = sb("wd", [P, 2, D_OUT])
        wd_sum = sb("wd_sum", [P, 2])
        wd_mean = sb("wd_mean", [P, 2])
        w1 = sb("w1", [P, 5, D_H1])
        w2 = sb("w2", [P, 4, D_H2])
        w3 = sb("w3", [P, 2])
        cols = sb("cols", [P, 15])
        b1, b2 = cols[:, 0:4], cols[:, 4:6]
        gl, bl = cols[:, 6:9], cols[:, 9:12]
        gd, bd, bs = cols[:, 12:13], cols[:, 13:14], cols[:, 14:15]
        eps = sb("eps", [P, 1])

        ids = sb("ids", [P, TILES, GATHERS], I32)
        base = sb("base", [P, GATHERS], I32)
        rows = sb("rows", [P, TILES * GATHERS], I32)
        idx = [sb(f"idx{i}", [P, GATHERS], I32) for i in range(2)]
        emb = [sb(f"emb{i}", [P, GATHERS, D_EMB]) for i in range(2)]
        emb_t = sb("emb_t", [P, KT, P])
        prod = sb("prod", [P, 2 * len(K_OF[0]), D_EMB])
        q = sb("q", [P, GATHERS])
        q_sd = sb("q_sd", [P, GATHERS])
        q_rstd = sb("q_rstd", [P, GATHERS])
        emb_n = sb("emb_n", [P, GATHERS, D_EMB])
        v = sb("v", [P, CHUNKS, CS * N_PROJ])
        yb = [sb(f"yb{i}", [P, CS, N_PROJ]) for i in range(2)]
        sq = [sb(f"sq{i}", [P, CS, N_PROJ]) for i in range(2)]
        ss = sb("ss", [P, CHUNKS, 2, CS])
        y_sd = sb("y_sd", [P, CHUNKS, 2, CS])
        y_rstd = sb("y_rstd", [P, CHUNKS, 2, CS])
        feat = [sb(f"feat{i}", [P, TILE, N_FEAT]) for i in range(2)]
        zc = [sb(f"zc{i}", [P, N_BLOCKS, GROUPS, QC]) for i in range(2)]
        zs = [sb(f"zs{i}", [PAIR_ROWS, GRP, GROUPS, QC]) for i in range(2)]
        dense_x = [sb(f"dense_x{i}", [P, 2, TILE]) for i in range(2)]
        dense_h = [sb(f"dense_h{i}", [P, 2, TILE]) for i in range(2)]
        x_raw = sb("x_raw", [P, D_OUT])
        x_junk = sb("x_junk", [P, D_OUT])
        x_stat = sb("x_stat", [P, 3])
        x_n = sb("x_n", [P, D_OUT])
        o_junk = sb("o_junk", [P, D_PAIR])
        o_stat = sb("o_stat", [P, 3])
        o_n = sb("o_n", [P, D_USED])
        h0 = sb("h0", [P, 3, TILE])
        h1 = sb("h1", [P, 4, TILE])
        h2 = sb("h2", [P, 2, TILE])
        y_all = sb("y_all", [P, TILES])

        pa, pw, pv = bank("pa"), bank("pw"), bank("pv")
        pt = [bank("pt0"), bank("pt1")]
        pz, po, ph = bank("pz"), bank("po"), bank("ph")

        early_loaded, pairs_loaded, late_loaded = sem("early_loaded"), sem("pairs_loaded"), sem("late_loaded")
        wl_loaded = sem("wl_loaded")
        ids_loaded = sem("ids_loaded")
        gathered = [[sem(f"gathered{i}_{c}") for c in range(CHUNKS)] for i in range(2)]
        dense_x_loaded = [sem(f"dense_x_loaded{i}") for i in range(2)]
        dense_h_loaded = [sem(f"dense_h_loaded{i}") for i in range(2)]
        zs_loaded = [sem(f"zs_loaded{i}") for i in range(2)]
        dots_stored = [sem(f"dots_stored{i}") for i in range(2)]
        out_stored = sem("out_stored")
        rows_ready, idx_ready, chunk_open = sem("rows_ready"), sem("idx_ready"), sem("chunk_open")
        prep_pe, prep_dve = sem("prep_pe"), sem("prep_dve")
        fold_pe, fold_dve, fold_act = sem("fold_pe"), sem("fold_dve"), sem("fold_act")
        emb_t_done, w_done, v_done, t_done = sem("emb_t_done"), sem("w_done"), sem("v_done"), sem("t_done")
        z_done, o_done, ot_done, x_done = sem("z_done"), sem("o_done"), sem("ot_done"), sem("x_done")
        h1_done, h2_done, xt_done, y_done = sem("h1_done"), sem("h2_done"), sem("xt_done"), sem("y_done")
        emb_t_ready, v_ready, sq_ready = sem("emb_t_ready"), sem("v_ready"), sem("sq_ready")
        q_sd_ready, y_sd_ready = sem("q_sd_ready"), sem("y_sd_ready")
        x_raw_ready, x_ss_ready, x_sd_ready, x_n_ready, x_ready = (
            sem("x_raw_ready"), sem("x_ss_ready"), sem("x_sd_ready"), sem("x_n_ready"), sem("x_ready"))
        o_ss_ready, o_sd_ready, o_n_ready = sem("o_ss_ready"), sem("o_sd_ready"), sem("o_n_ready")
        zc_ready, h0_ready, h2_ready = sem("zc_ready"), sem("h0_ready"), sem("h2_ready")
        h1_ready, y_ready = sem("h1_ready"), sem("y_ready")
        prod_ready, q_ready, q_rstd_ready, emb_n_ready = sem("prod_ready"), sem("q_ready"), sem("q_rstd_ready"), sem("emb_n_ready")
        yb_ready = sem("yb_ready")
        ss_ready, y_rstd_ready, feat_ready = sem("ss_ready"), sem("y_rstd_ready"), sem("feat_ready")
        x_rstd_ready, o_rstd_ready = sem("x_rstd_ready"), sem("o_rstd_ready")

        EARLY, PAIRS, LATE = 9, 2, 3
        N_PREP = 9
        N_FOLD = 4 + QC

        block = ctx.enter_context(nc.Block())

        @block.sync
        def _(sp):
            sp.dma_start(ids[:], d["ids_t"]).then_inc(ids_loaded, 16)
            sp.dma_start(base[:], d["table_base"]).then_inc(ids_loaded, 16)
            sp.dma_start(wl[:], d["wl_pair"]).then_inc(wl_loaded, 16)
            for to, src in ((wsi_raw[:], d["wsi_k"]), (wsi_mask[:], d["wsi_mask"]), (cols[:], d["cols"])):
                sp.dma_start(to, src).then_inc(early_loaded, 16)
            for to, src in ((pair_gb[:], d["pair_gb"]), (pair_mask[:], d["pair_mask"])):
                sp.dma_start(to, src).then_inc(pairs_loaded, 16)
            sp.wait_ge(gathered[0][0], 16 * 2 * len(K_OF[0]))
            for to, src in ((w1[:], d["w1_k"]), (w2[:], d["w2_k"]), (w3[:], d["w3_k"])):
                sp.dma_start(to, src).then_inc(late_loaded, 16)

            def step(s):
                if s.live(1):
                    wait(sp, zc_ready, s.count(1, CHUNKS, CHUNKS))
                    sp.dma_start(dots[s.slot(1)], zc[s.slot(1)][:].rearrange("p b g q -> p b (g q)")).then_inc(dots_stored[s.slot(1)], 16)
                    sp.wait_ge(dots_stored[s.slot(1)], (s.visits(1) + 1) * 16)
                    for b, (_, _, n) in enumerate(BLOCKS):
                        sp.dma_start(zs[s.slot(1)][PAIR_AT[b]:PAIR_AT[b] + n].rearrange("p j g q -> p j (g q)"),
                                     dots[s.slot(1)].rearrange("(j r) b x -> b r j x", j=GRP)[b, 0:n]
                                     ).then_inc(zs_loaded[s.slot(1)], 16)

            run_steps(sp, step)
            sp.wait_ge(y_ready, TILES)
            sp.dma_start(y_out, y_all[:]).then_inc(out_stored, 16)
            sp.wait_ge(out_stored, 16)

        @block.gpsimd
        def _(pool):
            pool.wait_ge(ids_loaded, 32)
            nc.gpsimd.tensor_tensor(rows[:].rearrange("p (t g) -> p t g", t=TILES), ids[:],
                                    base[:].unsqueeze(1).to_broadcast([P, TILES, GATHERS]), ALU.add).then_inc(rows_ready, 1)
            pool.wait_ge(rows_ready, 1)

            def step(s):
                if not s.live(0):
                    return
                for c in range(CHUNKS):
                    wait(pool, gathered[s.slot(0)][c], s.visits(0) * (16 * 2 * len(K_OF[c])))
                nc.gpsimd.tensor_copy(idx[s.slot(0)][:], rows[:, bass.ds(s.tile(0) * GATHERS, GATHERS)]).then_inc(idx_ready, 1)
                pool.wait_ge(idx_ready, s.count(0, 1, 1))
                for c in range(CHUNKS):
                    wait(pool, emb_n_ready, s.count(0, CHUNKS, c + 1 - 2 * CHUNKS))
                    pool.sem_inc(chunk_open)
                    for g in range(2 * K_OF[c][0], 2 * K_OF[c][-1] + 2):
                        pool.indirect_dma_start(
                            emb[s.slot(0)][:, g], None, d["tables"],
                            bass.IndirectOffsetOnAxis(ap=idx[s.slot(0)][:, g:g + 1], axis=0),
                        ).then_inc(gathered[s.slot(0)][c], 16)

            run_steps(pool, step)

        @block.scalar
        def _(act):
            for to, src in ((ident[:], d["ident"]), (centre[:], d["centre"]), (ws2[:, 0], d["Ws"]), (ws2[:, 1], d["Ws"]),
                            (gs_b[:], d["gs"].to_broadcast([P, D_OUT])), (wd[:], d["wd_t"])):
                act.dma_start(to, src).then_inc(early_loaded, 16)
            act.wait_ge(wl_loaded, 16)
            for k in range(QC):
                last = nc.scalar.activation(wl_junk[:, k], wl[:, k], ACT.Copy, accum_out=wl_sum[:, k:k + 1])
            last.then_inc(fold_act, 1)
            act.wait_ge(fold_act, 1)
            nc.scalar.activation(wl_mean[:], wl_sum[:], ACT.Copy, scale=-1.0 / D_PAIR).then_inc(fold_act, 1)
            act.wait_ge(fold_act, 2)
            for k in range(QC):
                last = nc.scalar.activation(wl[:, k], wl[:, k], ACT.Identity, bias=wl_mean[:, k:k + 1])
            last.then_inc(fold_act, 1)

            def scale_pairs(c):
                if c < CHUNKS - 1:
                    act.wait_ge(fold_pe, 1)
                    for k in range(2 * c, min(2 * c + 2, QC)):
                        nc.scalar.activation(wl[:, k], wl[:, k], ACT.Copy, scale=pair_gg[:, k:k + 1]).then_inc(fold_act, 1)
                else:
                    act.wait_ge(fold_act, 3 + QC)
                    nc.scalar.copy(wl[0:N_COL, QC - 1], po[0:N_COL]).then_inc(fold_act, 1)

            act.wait_ge(prep_dve, 1)

            def step(s):
                if s.live(0):
                    wait(act, x_done, s.count(0, 1, -1))
                    act.dma_start(dense_x[s.slot(0)][:], d["dense_t"][s.tile(0)]).then_inc(dense_x_loaded[s.slot(0)], 16)
                if s.live(3):
                    act.dma_start(dense_h[s.slot(3)][:], d["dense_t"][s.tile(3)]).then_inc(dense_h_loaded[s.slot(3)], 16)
                for c in range(CHUNKS):
                    lm, cm = mixed(c)
                    if s.live(0):
                        wait(act, emb_t_done, s.count(0, CHUNKS, c + 1))
                        wait(act, w_done, s.count(0, CHUNKS, c + 1 - CHUNKS))
                        nc.scalar.copy(emb_t[:, K_OF[c][0]:K_END[c]].rearrange("p k r -> p (k r)"), pa[:, 0:P * len(K_OF[c])]).then_inc(emb_t_ready, 1)
                    if s.live(lm):
                        wait(act, v_done, s.count(lm, CHUNKS, cm + 1))
                        wait(act, t_done, s.count(lm, 2 * CHUNKS, 2 * cm + 2 - 2 * CHUNKS))
                        nc.scalar.copy(v[:, cm], pv[:]).then_inc(v_ready, 1)
                    if s.live(0) and c == 1:
                        wait(act, x_done, s.count(0, 1, 1))
                        wait(act, x_n_ready, s.count(0, 1, 0))
                        nc.scalar.copy(x_raw[:], ph[:, 384:512]).then_inc(x_raw_ready, 1)
                        wait(act, x_raw_ready, s.count(0, 1, 1))
                        wait(act, x_rstd_ready, s.count(0, 1, 0))
                        nc.scalar.activation(x_junk[:], x_raw[:], ACT.Square, accum_out=x_stat[:, 0:1]).then_inc(x_ss_ready, 1)
                    if s.live(0) and c == 2:
                        wait(act, x_rstd_ready, s.count(0, 1, 1))
                        wait(act, xt_done, s.count(0, 1, 0))
                        nc.scalar.activation(x_n[:], x_raw[:], ACT.Copy, scale=x_stat[:, 2:3]).then_inc(x_n_ready, 1)
                    if s.live(1 if c == 0 else 0):
                        at, b = (1, CHUNKS - 1) if c == 0 else (0, c - 1)
                        wait(act, q_ready, s.count(at, CHUNKS, b + 1))
                        wait(act, q_rstd_ready, s.count(at, CHUNKS, b + 1 - CHUNKS))
                        nc.scalar.activation(q_sd[:, gathers_of(b)], q[:, gathers_of(b)], ACT.Sqrt, bias=eps[:]).then_inc(q_sd_ready, 1)
                    if s.live(0) and c == 1:
                        wait(act, x_ss_ready, s.count(0, 1, 1))
                        nc.scalar.activation(x_stat[:, 1:2], x_stat[:, 0:1], ACT.Sqrt, bias=eps[:], scale=1.0 / D_OUT).then_inc(x_sd_ready, 1)
                    if s.live(3) and c == 0:
                        wait(act, o_done, s.count(3, 1, 1))
                        wait(act, o_n_ready, s.count(3, 1, 0))
                        nc.scalar.activation(o_junk[:], po[:], ACT.Square, accum_out=o_stat[:, 0:1]).then_inc(o_ss_ready, 1)
                        wait(act, o_ss_ready, s.count(3, 1, 1))
                        nc.scalar.activation(o_stat[:, 1:2], o_stat[:, 0:1], ACT.Sqrt, bias=eps[:], scale=1.0 / D_PAIR).then_inc(o_sd_ready, 1)
                        wait(act, o_rstd_ready, s.count(3, 1, 1))
                        wait(act, ot_done, s.count(3, 1, 0))
                        nc.scalar.activation(o_n[:], po[:, 0:D_USED], ACT.Copy, scale=o_stat[:, 2:3]).then_inc(o_n_ready, 1)
                    if s.live(1):
                        wait(act, z_done, s.count(1, CHUNKS, c + 1))
                        if c == 0:
                            wait(act, dots_stored[s.slot(1)], s.visits(1) * 16)
                        z = pz[:, 0:CG * N_COL].rearrange("p (g c) -> p g c", c=N_COL)
                        first = BLOCKS[0][1]
                        nc.scalar.copy(zc[s.slot(1)][:, 0, CG * c:CG * (c + 1), 0:first], z[:, :, 0:first])
                        nc.scalar.copy(zc[s.slot(1)][:, 1:, CG * c:CG * (c + 1)],
                                       z[:, :, first:].rearrange("p g (b q) -> p b g q", q=QC)).then_inc(zc_ready, 1)
                    if s.live(lm):
                        for h in range(2):
                            n = 2 * cm + h
                            wait(act, yb_ready, s.count(lm, 2 * CHUNKS, n + 1))
                            wait(act, ss_ready, s.count(lm, 2 * CHUNKS, n - 1))
                            nc.scalar.activation(sq[h][:], yb[h][:], ACT.Square).then_inc(sq_ready, 1)
                    if c == 0:
                        if s.live(0):
                            wait(act, x_done, s.count(0, 1, 1))
                        if s.live(3):
                            wait(act, ot_done, s.count(3, 1, 1))
                            for k in range(3):
                                last = nc.scalar.activation(h0[:, k], ph[:, P * k:P * (k + 1)], ACT.Identity,
                                                            bias=bl[:, k:k + 1], scale=gl[:, k:k + 1])
                            last.then_inc(h0_ready, 1)
                    if s.live(lm):
                        wait(act, ss_ready, s.count(lm, 2 * CHUNKS, 2 * cm + 2))
                        wait(act, y_rstd_ready, s.count(lm, CHUNKS, cm + 1 - CHUNKS))
                        nc.scalar.activation(y_sd[:, cm], ss[:, cm], ACT.Sqrt, bias=eps[:], scale=1.0 / N_PROJ).then_inc(y_sd_ready, 1)
                    if c == 2:
                        if s.live(0):
                            wait(act, xt_done, s.count(0, 1, 1))
                        if s.live(3):
                            wait(act, h2_done, s.count(3, 1, 1))
                            for m in range(2):
                                last = nc.scalar.activation(h2[:, m], ph[:, P * m:P * (m + 1)], ACT.Relu, bias=b2[:, m:m + 1])
                            last.then_inc(h2_ready, 1)
                        if s.live(0):
                            if s.fixed and s.tile(0) == 0:
                                act.wait_ge(early_loaded, 16 * EARLY)
                            wait(act, z_done, s.count(0, CHUNKS, -CHUNKS))
                            nc.scalar.activation(feat[s.slot(0)][:].rearrange("p (g j) f -> p j g f", j=GRP)[:, :, :, 0],
                                                 ph[:, 384:512].rearrange("p (j g) -> p j g", j=GRP), ACT.Identity,
                                                 bias=bd, scale=gd).then_inc(x_ready, 1)
                    if s.fixed and s.live(0) and s.tile(0) == 1:
                        scale_pairs(c)
            run_steps(act, step)

        @block.vector
        def _(dve):
            links = [0]

            def link(ins):
                links[0] += 1
                ins.then_inc(prep_dve, 1)
                dve.wait_ge(prep_dve, links[0])

            nc.vector.memset(eps[:], EPS)
            nc.vector.memset(ones[:], 1.0)
            link(nc.vector.memset(gram[:], 0.0))
            dve.wait_ge(early_loaded, 16 * EARLY)
            link(nc.vector.reduce_sum(wsi_sum[:], wsi_raw[:], AX))
            link(nc.vector.tensor_scalar(wsi_mean[:], wsi_sum[:], -1.0 / N_PROJ, None, ALU.mult))
            link(nc.vector.tensor_tensor(wsi_c[:], wsi_raw[:], wsi_mean[:].unsqueeze(2).to_broadcast([P, KT, N_PROJ]), ALU.add))
            dve.wait_ge(prep_pe, 1)
            link(nc.vector.tensor_copy(wc2[:], pa[:, 0:P]))
            dve.wait_ge(prep_pe, 2)
            nc.vector.tensor_tensor(wg_t[:], pw[:, 0:P], gs_b[:], ALU.mult)
            nc.vector.tensor_tensor(wsi[:], wsi_c[:].unsqueeze(2).to_broadcast([P, KT, TOUCH, N_PROJ]),
                                    wsi_mask[:].unsqueeze(3).to_broadcast([P, KT, TOUCH, N_PROJ]), ALU.mult)
            dve.wait_ge(prep_pe, 3)
            for h in range(2):
                rows_h = slice(D_EMB * h, D_EMB * (h + 1))
                nc.vector.tensor_scalar(gram[rows_h, rows_h], pv[rows_h, 0:D_EMB], 1.0 / D_OUT, None, ALU.mult)
            dve.wait_ge(prep_pe, 4)
            link(nc.vector.tensor_scalar(y_bias[:], pz[:, 0:N_PROJ], bs, None, ALU.mult))
            link(nc.vector.reduce_sum(wd_sum[:], wd[:], AX))
            link(nc.vector.tensor_scalar(wd_mean[:], wd_sum[:], 1.0 / D_OUT, None, ALU.mult))
            for k in range(2):
                last = nc.vector.tensor_scalar(wd[:, k], wd[:, k], wd_mean[:, k:k + 1], None, ALU.subtract)
            link(last)
            for i in range(2):
                nc.vector.memset(feat[i][:, :, N_PROJ + 1:N_FEAT], 1.0)
                nc.vector.memset(zc[i][:, 0, :, BLOCKS[0][1]:QC], 1.0)

            folds = [0]

            def fold_link(ins):
                folds[0] += 1
                ins.then_inc(fold_dve, 1)
                dve.wait_ge(fold_dve, folds[0])

            dve.wait_ge(pairs_loaded, 16 * PAIRS)
            g_row, b_row, g_col, b_col = (pair_gb[:, k] for k in range(4))
            nc.vector.tensor_tensor(pair_gg[:], g_row, g_col, ALU.mult)
            nc.vector.tensor_tensor(pair_coef[:, 0], b_col, g_row, ALU.mult)
            nc.vector.tensor_tensor(pair_coef[:, 1], b_row, g_col, ALU.mult)
            fold_link(nc.vector.tensor_tensor(pair_coef[:, 2], b_row, b_col, ALU.mult))
            fold_link(nc.vector.tensor_tensor(fold_parts[:], pair_mask[:],
                                             pair_coef[:].unsqueeze(3).to_broadcast([PAIR_ROWS, 3, QC, N_COL]), ALU.mult))
            fold_link(nc.vector.tensor_tensor(fold_two[:], fold_parts[:, 0], fold_parts[:, 1], ALU.add))
            fold_link(nc.vector.tensor_tensor(fold[:], fold_two[:], fold_parts[:, 2], ALU.add))

            def step(s):
                for c in range(CHUNKS):
                    lm, cm = mixed(c)
                    if s.live(1 if c == 0 else 0):
                        at, b = (1, CHUNKS - 1) if c == 0 else (0, c - 1)
                        g = gathers_of(b)
                        wait(dve, q_sd_ready, s.count(at, CHUNKS, b + 1))
                        nc.vector.reciprocal(q_rstd[:, g], q_sd[:, g]).then_inc(q_rstd_ready, 1)
                        wait(dve, q_rstd_ready, s.count(at, CHUNKS, b + 1))
                        wait(dve, v_done, s.count(at, CHUNKS, min(b + 2, CHUNKS) - CHUNKS))
                        nc.vector.tensor_tensor(emb_n[:, g], emb[s.slot(at)][:, g],
                                                q_rstd[:, g].unsqueeze(2).to_broadcast([P, 2 * len(K_OF[b]), D_EMB]),
                                                ALU.mult).then_inc(emb_n_ready, 1)
                    if s.live(3) and c == 0:
                        wait(dve, o_sd_ready, s.count(3, 1, 1))
                        nc.vector.reciprocal(o_stat[:, 2:3], o_stat[:, 1:2]).then_inc(o_rstd_ready, 1)
                    if s.live(lm):
                        for h in range(2):
                            wait(dve, feat_ready, s.count(lm, 2 * CHUNKS, 2 * cm + h - 1))
                            wait(dve, t_done, s.count(lm, 2 * CHUNKS, 2 * cm + h + 1))
                            nc.vector.tensor_tensor(yb[h][:], pt[h][:].rearrange("p (b f) -> p b f", b=CS),
                                                    y_bias[:].unsqueeze(1).to_broadcast([P, CS, N_PROJ]), ALU.add).then_inc(yb_ready, 1)
                        for h in range(2):
                            wait(dve, sq_ready, s.count(lm, 2 * CHUNKS, 2 * cm + h + 1))
                            wait(dve, y_sd_ready, s.count(lm, CHUNKS, cm + 1 - CHUNKS))
                            nc.vector.reduce_sum(ss[:, cm, h], sq[h][:], AX).then_inc(ss_ready, 1)
                    if s.live(0) and c == 1:
                        wait(dve, x_sd_ready, s.count(0, 1, 1))
                        nc.vector.reciprocal(x_stat[:, 2:3], x_stat[:, 1:2]).then_inc(x_rstd_ready, 1)
                    if s.live(0):
                        n = 2 * len(K_OF[c])
                        wait(dve, w_done, s.count(0, CHUNKS, c + 1))
                        nc.vector.tensor_tensor(prod[:, 0:n], pw[:, 0:n * D_EMB].rearrange("p (a b) -> p a b", b=D_EMB),
                                                emb[s.slot(0)][:, gathers_of(c)], ALU.mult).then_inc(prod_ready, 1)
                    if s.live(lm):
                        wait(dve, y_sd_ready, s.count(lm, CHUNKS, cm + 1))
                        nc.vector.reciprocal(y_rstd[:, cm], y_sd[:, cm]).then_inc(y_rstd_ready, 1)
                    if s.live(0):
                        wait(dve, prod_ready, s.count(0, CHUNKS, c + 1))
                        wait(dve, q_sd_ready, s.count(0, CHUNKS, c + 1 - CHUNKS))
                        nc.vector.reduce_sum(q[:, gathers_of(c)], prod[:, 0:2 * len(K_OF[c])], AX).then_inc(q_ready, 1)
                    if s.live(lm):
                        wait(dve, y_rstd_ready, s.count(lm, CHUNKS, cm + 1))
                        if cm == 0:
                            wait(dve, z_done, s.count(lm, CHUNKS, -CHUNKS))
                        for h in range(2):
                            at = CG * GRP * cm + CS * h
                            nc.vector.tensor_tensor(feat[s.slot(lm)][:, at:at + CS, 1:1 + N_PROJ], yb[h][:],
                                                    y_rstd[:, cm, h].unsqueeze(2).to_broadcast([P, CS, N_PROJ]),
                                                    ALU.mult).then_inc(feat_ready, 1)
                    if c == 1 and s.live(3):
                        wait(dve, h1_done, s.count(3, 1, 1))
                        for m in range(4):
                            last = nc.vector.tensor_scalar(h1[:, m], ph[:, P * m:P * (m + 1)], b1[:, m:m + 1], 0.0, ALU.add, ALU.max)
                        last.then_inc(h1_ready, 1)
                    if c == 3 and s.live(3):
                        wait(dve, y_done, s.count(3, 1, 1))
                        nc.vector.tensor_copy(y_all[:, bass.ds(s.tile(3), 1)], ph[:, 0:1]).then_inc(y_ready, 1)

            run_steps(dve, step)

        @block.tensor
        def _(pe):
            pe.wait_ge(early_loaded, 16 * EARLY)
            ws_flat = ws2[:].rearrange("p h d -> p (h d)")
            nc.tensor.matmul(pa[:, 0:P], centre[:], ws_flat, start=True, stop=True).then_inc(prep_pe, 1)
            nc.tensor.matmul(pw[:, 0:P], ws_flat, centre[:], start=True, stop=True).then_inc(prep_pe, 1)
            pe.wait_ge(prep_dve, 5)
            nc.tensor.matmul(pv[:, 0:D_EMB], wc2[:], wc2[:, 0:D_EMB], start=True, stop=True).then_inc(prep_pe, 1)
            nc.tensor.matmul(pz[:, 0:N_PROJ], ones[:], wsi_c[0:N_TABLES, 0], start=True, stop=True).then_inc(prep_pe, 1)

            PROJECT = {2: range(0, 2), 3: range(2, QC)}

            def step(s):
                for c in range(CHUNKS):
                    lm, cm = mixed(c)
                    if s.live(0):
                        pe.wait_ge(gathered[s.slot(0)][c], (s.visits(0) + 1) * (16 * 2 * len(K_OF[c])))
                        wait(pe, emb_t_ready, s.count(0, CHUNKS, c))
                        for a, k in enumerate(K_OF[c]):
                            last = nc.tensor.transpose(pa[:, P * a:P * (a + 1)],
                                                       emb[s.slot(0)][:, 2 * k:2 * k + 2].rearrange("p g d -> p (g d)"), ident[:])
                        last.then_inc(emb_t_done, 1)
                    if s.live(lm):
                        wait(pe, emb_n_ready, s.count(lm, CHUNKS, cm + 1))
                        wait(pe, v_ready, s.count(lm, CHUNKS, cm))
                        places = mix_places(cm)
                        for k, place, b, n in places:
                            last = nc.tensor.matmul(pv[:, N_PROJ * b:N_PROJ * (b + n)], emb_n[:, 2 * k:2 * k + 2].rearrange("p g d -> p (g d)"),
                                                    wsi[:, k, place:place + n].rearrange("p b f -> p (b f)"),
                                                    start=(k == places[0][0]), stop=(k == places[-1][0]), skip_group_check=True)
                        last.then_inc(v_done, 1)
                    if s.live(1):
                        wait(pe, feat_ready, s.count(1, 2 * CHUNKS, 2 * c + 2))
                        if c == 0:
                            wait(pe, x_ready, s.count(1, 1, 1))
                        wait(pe, zc_ready, s.count(1, CHUNKS, c))
                        for g in range(CG):
                            for j in range(GRP):
                                t = feat[s.slot(1)][:, GRP * (CG * c + g) + j]
                                last = nc.tensor.matmul(pz[32 * j:32 * j + 32, N_COL * g:N_COL * (g + 1)], t[:, 0:N_PROJ], t[:, 1:N_FEAT],
                                                        start=True, stop=True)
                        last.then_inc(z_done, 1)
                    if s.live(lm):
                        wait(pe, v_ready, s.count(lm, CHUNKS, cm + 1))
                        for h in range(2):
                            wait(pe, yb_ready, s.count(lm, 2 * CHUNKS, 2 * cm + h - 1))
                            hd = slice(D_EMB * h, D_EMB * (h + 1))
                            nc.tensor.matmul(pt[h][:], wg_t[hd, :], v[hd, cm], start=True, stop=True).then_inc(t_done, 1)
                    if s.live(0):
                        if s.fixed and s.tile(0) == 0 and c == 0:
                            pe.wait_ge(prep_dve, 6)
                        wait(pe, emb_t_ready, s.count(0, CHUNKS, c + 1))
                        wait(pe, prod_ready, s.count(0, CHUNKS, c))
                        for a, k in enumerate(K_OF[c]):
                            last = nc.tensor.matmul(pw[:, P * a:P * (a + 1)], emb_t[:, k], gram[:], start=True, stop=True)
                        last.then_inc(w_done, 1)
                    if s.fixed and s.live(0) and s.tile(0) == 0 and c < 2:
                        pe.wait_ge(fold_dve, 4)
                        pe.wait_ge(fold_act, 3)
                        for k in range(3 * c, min(3 * c + 3, QC)):
                            last = nc.tensor.matmul(po[0:N_COL], fold[:, k], wl[:, k], start=(k == 0), stop=(k == QC - 1))
                        if c == 1:
                            last.then_inc(fold_pe, 1)
                    if s.live(2) and c >= 2:
                        if c == 2:
                            if s.fixed and s.tile(2) == 0:
                                pe.wait_ge(fold_act, N_FOLD)
                            pe.wait_ge(zs_loaded[s.slot(2)], (s.visits(2) + 1) * (16 * N_BLOCKS))
                            wait(pe, o_n_ready, s.count(2, 1, 0))
                        for k in PROJECT[c]:
                            last = nc.tensor.matmul(po[:], zs[s.slot(2)][:].rearrange("p j g q -> p (j g) q")[:, :, k], wl[:, k],
                                                    start=(k == 0), stop=(k == QC - 1))
                        if c == 3:
                            last.then_inc(o_done, 1)
                    if c == 0:
                        if s.live(4):
                            wait(pe, y_ready, s.count(4, 1, 1))
                        if s.live(1):
                            wait(pe, x_ready, s.count(1, 1, 1))
                        if s.live(3):
                            wait(pe, o_n_ready, s.count(3, 1, 1))
                            for k in range(3):
                                last = nc.tensor.transpose(ph[:, P * k:P * (k + 1)], o_n[:, P * k:P * (k + 1)], ident[:])
                            last.then_inc(ot_done, 1)
                        if s.live(0):
                            if s.fixed and s.tile(0) == 0:
                                pe.wait_ge(prep_dve, N_PREP)
                            pe.wait_ge(dense_x_loaded[s.slot(0)], (s.visits(0) + 1) * 16)
                            for k in range(2):
                                last = nc.tensor.matmul(ph[:, 384:512], dense_x[s.slot(0)][:, k], wd[:, k], start=(k == 0), stop=(k == 1))
                            last.then_inc(x_done, 1)
                    if c == 1 and s.live(3):
                        if s.fixed and s.tile(3) == 0:
                            pe.wait_ge(late_loaded, 16 * LATE)
                        wait(pe, h0_ready, s.count(3, 1, 1))
                        if s.live(0):
                            wait(pe, x_raw_ready, s.count(0, 1, 1))
                        pe.wait_ge(dense_h_loaded[s.slot(3)], (s.visits(3) + 1) * 16)
                        for m in range(4):
                            for k in range(5):
                                rhs = h0[:, k] if k < 3 else dense_h[s.slot(3)][:, k - 3]
                                last = nc.tensor.matmul(ph[:, P * m:P * (m + 1)], w1[:, k, P * m:P * (m + 1)], rhs, start=(k == 0), stop=(k == 4))
                        last.then_inc(h1_done, 1)
                    if c == 2:
                        if s.live(3):
                            wait(pe, h1_ready, s.count(3, 1, 1))
                            for m in range(2):
                                for k in range(4):
                                    last = nc.tensor.matmul(ph[:, P * m:P * (m + 1)], w2[:, k, P * m:P * (m + 1)], h1[:, k], start=(k == 0), stop=(k == 3))
                            last.then_inc(h2_done, 1)
                        if s.live(0):
                            wait(pe, x_raw_ready, s.count(0, 1, 1))
                            wait(pe, x_n_ready, s.count(0, 1, 1))
                            nc.tensor.transpose(ph[:, 384:512], x_n[:], ident[:]).then_inc(xt_done, 1)
                    if c == 3 and s.live(3):
                        wait(pe, h2_ready, s.count(3, 1, 1))
                        if s.live(0):
                            wait(pe, x_ready, s.count(0, 1, 1))
                        for k in range(2):
                            last = nc.tensor.matmul(ph[:, 0:1], h2[:, k], w3[:, k:k + 1], start=(k == 0), stop=(k == 1))
                        last.then_inc(y_done, 1)

            run_steps(pe, step)


def constants():
    ident = np.eye(P, dtype=np.float32)
    centre = (np.eye(P) - 1.0 / P).astype(np.float32)
    sample = (P * np.arange(KT) + np.arange(P)[:, None]) // N_TABLES
    mask = (sample[:, :, None] == P * np.arange(KT)[:, None] // N_TABLES + np.arange(TOUCH)).astype(np.float32)
    return ident, centre, mask


def pair_layout():
    row = np.zeros(PAIR_ROWS, int)
    col = np.full((PAIR_ROWS, QC), N_COL)
    for b, (first, n_cols, n_rows) in enumerate(BLOCKS):
        at = slice(PAIR_AT[b], PAIR_AT[b] + n_rows)
        row[at] = np.arange(n_rows)
        col[at, :n_cols] = first + np.arange(n_cols)
    return row, col


def pair_mask(row, col):
    mask = np.zeros((PAIR_ROWS, 3, QC, N_COL), np.float32)
    r = np.arange(N_PROJ)
    mask[:, 0, :, :N_PROJ] = row[:, None, None] == r
    mask[:, 1, :, :N_PROJ] = col[:, :, None] == r
    mask[:, 1, :, 1:N_PROJ] -= (col == N_PROJ)[:, :, None]
    mask[:, 2, :, N_PROJ] = D_OUT
    return mask


def kernel(**inputs):
    import concourse.bacc as bacc
    from concourse.bass_utils import run_bass_kernel_spmd as run

    a = {k: np.asarray(v) for k, v in inputs.items()}
    tables = [a[f"tbl_{i}"] for i in range(N_TABLES)]
    first = np.cumsum([0] + [len(t) for t in tables[:-1]]).astype(np.int32)
    ident, centre, mask = constants()
    table = (P * np.arange(KT) + np.arange(P)[:, None]) % N_TABLES
    pi, pj = np.tril_indices(N_PROJ + 1, k=-1)
    wl_full = np.zeros((N_PROJ + 1, N_COL + 1, D_PAIR), np.float32)
    wl_full[pj, pi] = a["L0_rec_Wl"].T
    row, col = pair_layout()
    wl_pair = wl_full[row[:, None], col]
    g_feat = np.concatenate([np.ones(1, np.float32), a["L0_rec_gsi"], np.ones(1, np.float32)])
    b_feat = np.concatenate([np.zeros(1, np.float32), a["L0_rec_bsi"], np.zeros(1, np.float32)])
    row_all = np.tile(row[:, None], (1, QC))
    pair_gb = np.stack([g_feat[row_all], b_feat[row_all], g_feat[col], b_feat[col]], axis=1)
    w_top1 = np.concatenate([a["W_top1"][:D_USED], a["W_top1"][D_PAIR:]])
    cols = np.concatenate([a["b_top1"].reshape(4, P).T, a["b_top2"].reshape(2, P).T,
                           a["L0_rec_gl"][:D_USED].reshape(3, P).T, a["L0_rec_bl"][:D_USED].reshape(3, P).T,
                           a["L0_rec_gd"][:, None], a["L0_rec_bd"][:, None], a["L0_rec_bs"][:, None]], axis=1)
    arrays = {
        "tables": np.concatenate(tables),
        "ids_t": a["ids"].reshape(TILES, 2, KT, P).transpose(3, 0, 2, 1).reshape(P, TILES, GATHERS),
        "table_base": np.repeat(first[table], 2, axis=1),
        "ident": ident, "centre": centre, "wsi_mask": mask,
        "Ws": a["L0_rec_Ws"], "gs": a["L0_rec_gs"][None],
        "wsi_k": a["L0_rec_Wsi"].T[table],
        "cols": cols, "pair_gb": pair_gb, "pair_mask": pair_mask(row, col), "wl_pair": wl_pair,
        "wd_t": a["L0_rec_Wd"].T.reshape(2, P, D_OUT).transpose(1, 0, 2),
        "w1_k": w_top1.reshape(5, P, D_H1).transpose(1, 0, 2),
        "w2_k": a["W_top2"].reshape(4, P, D_H2).transpose(1, 0, 2),
        "w3_k": a["W_top3"].reshape(2, P).T,
        "dense_t": a["r_dense_t"].reshape(TILES, 2, CHUNKS, GRP, GRP, 2, P).transpose(0, 6, 5, 4, 2, 1, 3).reshape(TILES, P, 2, TILE),
    }
    arrays = {k: np.ascontiguousarray(v) for k, v in arrays.items()}
    nc = bacc.Bacc("TRN2", target_bir_lowering=False, num_devices=1)
    d = {k: nc.dram_tensor("in_" + k, v.shape, mybir.dt.from_np(v.dtype), kind="ExternalInput").ap() for k, v in arrays.items()}
    y = nc.dram_tensor("y", (P, TILES), F32, kind="ExternalOutput").ap()
    dots = [nc.dram_tensor(f"dots{i}", (P, N_BLOCKS, GROUPS * QC), F32, kind="Internal").ap() for i in range(2)]
    build(nc, d, dots, y)
    r = run(nc, [{"in_" + k: v for k, v in arrays.items()}], core_ids=[0])
    return r.results[0]["y"].reshape(GRP, CHUNKS, 2, GRP, TILES).transpose(4, 2, 1, 3, 0).reshape(N_SAMPLES, 1)
```
